# Optimizing a Trainium2 kernel written in Bass

```python
import numpy as np
import jax
import jax.numpy as jnp

def _softmax(x, axis=-1):
    return jax.nn.softmax(x, axis=axis)

def _gelu(x):
    return jax.nn.gelu(x, approximate=True)

def _silu(x):
    return jax.nn.silu(x)

def _sigmoid(x):
    return jax.nn.sigmoid(x)

def _layernorm(x, axis=-1, eps=1e-05):
    m = jnp.mean(x, axis=axis, keepdims=True)
    v = jnp.var(x, axis=axis, keepdims=True)
    return (x - m) / jnp.sqrt(v + eps)

def _scatter_add(tgt, idx, src, axis=0):
    return tgt.at[idx].add(src)

def _segment_sum(src, seg, n):
    return jax.ops.segment_sum(src, seg, n)
kernel_name = 'mk_gnn_resnorm_d2_gnn_r8_adb0f5'

def setup_inputs(seed: int=0):
    np.random.seed(seed)
    _w = jnp.asarray

    def _rec_inputs():
        import jax
        import jax.numpy as jnp
        _gk = jax.random.key(seed)
        x = -1.686e-05 + 1 * jax.random.normal(jax.random.fold_in(_gk, 1), (6250, 160), jnp.float32)
        _s = jax.random.randint(jax.random.fold_in(_gk, 2), (50000,), 0, 6250, jnp.int32)
        _d = jax.random.randint(jax.random.fold_in(_gk, 3), (50000,), 0, 6250, jnp.int32)
        _loop = jnp.arange(6250, dtype=jnp.int32)
        src = jnp.concatenate([_s, _d, _loop])
        dst = jnp.concatenate([_d, _s, _loop])
        _o = jnp.argsort(dst, stable=True)
        src = src[_o]
        dst = dst[_o]
        edge_attr_4 = 0.0007022 + 0.999661 * jax.random.normal(jax.random.fold_in(_gk, 11), (106250, 4), jnp.float32)
        edge_attr_64 = 0.000196303 + 1.00016 * jax.random.normal(jax.random.fold_in(_gk, 12), (106250, 64), jnp.float32)
        node_vec1 = -0.00915711 + 0.999674 * jax.random.normal(jax.random.fold_in(_gk, 14), (6250, 1), jnp.float32)
        return (x, src, dst, edge_attr_4, edge_attr_64, node_vec1)
    x, src, dst, edge_attr_4, edge_attr_64, node_vec1 = _rec_inputs()

    def _L0_gnn_setup():
        import jax, jax.numpy as jnp
        import numpy as np
        N_NODES, N_EDGES = (6250, 50000)
        D, SPLIT, EA, H = (128, 32, 64, 256)
        IN = D + EA
        EPS = 1e-05
        SLOPE = 0.01

        def _ln(x, g, b):
            m = x.mean(-1, keepdims=True)
            v = ((x - m) ** 2).mean(-1, keepdims=True)
            return (x - m) * jax.lax.rsqrt(v + EPS) * g + b

        def _block(x, w, b, g, be):
            return jax.nn.relu(_ln(x @ w + b, g, be))

        def _masked_softmax(logits, mask):
            z = jnp.where(mask, logits, -jnp.inf)
            z = z - jnp.max(z, axis=0, keepdims=True)
            e = jnp.where(mask, jnp.exp(z), 0.0)
            return e / jnp.sum(e, axis=0, keepdims=True)

        def _forward(x, edge_index, edge_attr, w_att, b_att, d2t_w1, d2t_b1, d2t_g1, d2t_be1, d2t_w2, d2t_b2, d2t_g2, d2t_be2, t2d_w1, t2d_b1, t2d_g1, t2d_be1, t2d_w2, t2d_b2, t2d_g2, t2d_be2, node_w, node_b, node_g, node_be, self_w, self_b, self_g, self_be):
            x_split = x[:, D:]
            xn = x[:, :D]
            row, col = (edge_index[0], edge_index[1])
            n = xn.shape[0]
            concat = jnp.concatenate([xn[col], xn[row]], axis=-1)
            logits = jax.nn.leaky_relu(concat @ w_att + b_att, SLOPE)
            flow_in = jnp.concatenate([xn[col], edge_attr], axis=-1)

            def direction(mask, w1, b1, g1, be1, w2, b2, g2, be2):
                attn = _masked_softmax(logits, mask[:, None])
                h = attn * flow_in
                h = _block(h, w1, b1, g1, be1)
                h = _block(h, w2, b2, g2, be2)
                h = jnp.where(mask[:, None], h, 0.0)
                return jax.ops.segment_sum(h, row, num_segments=n)
            flow_d2t = direction(row < col, d2t_w1, d2t_b1, d2t_g1, d2t_be1, d2t_w2, d2t_b2, d2t_g2, d2t_be2)
            flow_t2d = direction(row > col, t2d_w1, t2d_b1, t2d_g1, t2d_be1, t2d_w2, t2d_b2, t2d_g2, t2d_be2)
            flow_total = jnp.concatenate([flow_t2d, flow_d2t], axis=1)
            upd = _block(flow_total, node_w, node_b, node_g, node_be)
            upd = upd + _block(xn, self_w, self_b, self_g, self_be)
            return jnp.concatenate([upd, x_split], axis=1)
        key = jax.random.key(seed)
        ks = jax.random.split(key, 24)

        def lin(k, fi, fo):
            kw, kb = jax.random.split(k)
            return (jax.random.normal(kw, (fi, fo), jnp.float32) / np.float32(np.sqrt(fi)), jax.random.normal(kb, (fo,), jnp.float32) * 0.02)

        def lnp(k, d):
            kg, kb = jax.random.split(k)
            return (1.0 + 0.05 * jax.random.normal(kg, (d,), jnp.float32), 0.05 * jax.random.normal(kb, (d,), jnp.float32))
        inp = {}
        inp['x'] = jax.random.normal(ks[0], (N_NODES, D + SPLIT), jnp.float32)
        inp['edge_index'] = jax.random.randint(ks[1], (2, N_EDGES), 0, N_NODES)
        inp['edge_attr'] = jax.random.normal(ks[2], (N_EDGES, EA), jnp.float32)
        inp['w_att'], inp['b_att'] = lin(ks[3], 2 * D, 1)
        for pre, off in (('d2t', 4), ('t2d', 10)):
            inp[pre + '_w1'], inp[pre + '_b1'] = lin(ks[off], IN, H)
            inp[pre + '_g1'], inp[pre + '_be1'] = lnp(ks[off + 1], H)
            inp[pre + '_w2'], inp[pre + '_b2'] = lin(ks[off + 2], H, D)
            inp[pre + '_g2'], inp[pre + '_be2'] = lnp(ks[off + 3], D)
        inp['node_w'], inp['node_b'] = lin(ks[16], 2 * D, D)
        inp['node_g'], inp['node_be'] = lnp(ks[17], D)
        inp['self_w'], inp['self_b'] = lin(ks[18], D, D)
        inp['self_g'], inp['self_be'] = lnp(ks[19], D)
        return inp
    _L0_gnn_all = _L0_gnn_setup()
    _L0_gnn_in = {k: v for k, v in _L0_gnn_all.items() if k in ('w_att', 'b_att', 'd2t_w1', 'd2t_b1', 'd2t_g1', 'd2t_be1', 'd2t_w2', 'd2t_b2', 'd2t_g2', 'd2t_be2', 't2d_w1', 't2d_b1', 't2d_g1', 't2d_be1', 't2d_w2', 't2d_b2', 't2d_g2', 't2d_be2', 'node_w', 'node_b', 'node_g', 'node_be', 'self_w', 'self_b', 'self_g', 'self_be')}
    del _L0_gnn_all

    def _L1_gnn_setup():
        import jax, jax.numpy as jnp
        import numpy as np
        MUL0, MUL1 = (64, 32)
        INV_SQRT3 = 1.0 / np.sqrt(3.0)

        def _split(x):
            return (x[:, :MUL0], x[:, MUL0:].reshape(x.shape[0], MUL1, 3))

        def _merge(o0, o1):
            return jnp.concatenate([o0, o1.reshape(o1.shape[0], -1)], axis=-1)

        def _tp(x0, x1, y0, y1, w000, w011, w101, w110):
            fan0 = x0.shape[1] * y0.shape[1] + x1.shape[1] * y1.shape[1]
            fan1 = x0.shape[1] * y1.shape[1] + x1.shape[1] * y0.shape[1]
            out0 = (jnp.einsum('eu,ev,uvw->ew', x0, y0, w000) + INV_SQRT3 * jnp.einsum('euk,evk,uvw->ew', x1, y1, w110)) / np.sqrt(fan0)
            out1 = (jnp.einsum('eu,evk,uvw->ewk', x0, y1, w011) + jnp.einsum('euk,ev,uvw->ewk', x1, y0, w101)) / np.sqrt(fan1)
            return (out0, out1)

        def _lin(x0, x1, w0, w1):
            return (x0 @ w0 / np.sqrt(x0.shape[1]), jnp.einsum('euk,uv->evk', x1, w1) / np.sqrt(x1.shape[1]))
        key = jax.random.key(seed)
        ks = jax.random.split(key, 20)
        N, E = (6250, 62500)
        inp = {'node_features': jax.random.normal(ks[0], (N, MUL0 + 3 * MUL1), dtype=jnp.float32), 'edge_index': jax.random.randint(ks[1], (2, E), 0, N, dtype=jnp.int64), 'edge_attr_tensor': jax.random.normal(ks[2], (E, 4), dtype=jnp.float32), 'node_attr_scalar_raw': jax.random.normal(ks[3], (N, 1), dtype=jnp.float32), 'wm000': jax.random.normal(ks[4], (MUL0, 1, MUL0), dtype=jnp.float32), 'wm011': jax.random.normal(ks[5], (MUL0, 1, MUL1), dtype=jnp.float32), 'wm101': jax.random.normal(ks[6], (MUL1, 1, MUL1), dtype=jnp.float32), 'wm110': jax.random.normal(ks[7], (MUL1, 1, MUL0), dtype=jnp.float32), 'lm0': jax.random.normal(ks[8], (MUL0, MUL0), dtype=jnp.float32), 'lm1': jax.random.normal(ks[9], (MUL1, MUL1), dtype=jnp.float32), 'wu000': jax.random.normal(ks[10], (MUL0, MUL0, MUL0), dtype=jnp.float32), 'wu011': jax.random.normal(ks[11], (MUL0, MUL1, MUL1), dtype=jnp.float32), 'wu101': jax.random.normal(ks[12], (MUL1, MUL0, MUL1), dtype=jnp.float32), 'wu110': jax.random.normal(ks[13], (MUL1, MUL1, MUL0), dtype=jnp.float32), 'lu0': jax.random.normal(ks[14], (MUL0, MUL0), dtype=jnp.float32), 'lu1': jax.random.normal(ks[15], (MUL1, MUL1), dtype=jnp.float32)}
        return inp
    _L1_gnn_all = _L1_gnn_setup()
    _L1_gnn_in = {k: v for k, v in _L1_gnn_all.items() if k in ('wm000', 'wm011', 'wm101', 'wm110', 'lm0', 'lm1', 'wu000', 'wu011', 'wu101', 'wu110', 'lu0', 'lu1')}
    del _L1_gnn_all
    return {'x': x, 'src': src, 'dst': dst, 'edge_attr_4': edge_attr_4, 'edge_attr_64': edge_attr_64, 'node_vec1': node_vec1, 'L0_gnn_w_att': _L0_gnn_in['w_att'], 'L0_gnn_b_att': _L0_gnn_in['b_att'], 'L0_gnn_d2t_w1': _L0_gnn_in['d2t_w1'], 'L0_gnn_d2t_b1': _L0_gnn_in['d2t_b1'], 'L0_gnn_d2t_g1': _L0_gnn_in['d2t_g1'], 'L0_gnn_d2t_be1': _L0_gnn_in['d2t_be1'], 'L0_gnn_d2t_w2': _L0_gnn_in['d2t_w2'], 'L0_gnn_d2t_b2': _L0_gnn_in['d2t_b2'], 'L0_gnn_d2t_g2': _L0_gnn_in['d2t_g2'], 'L0_gnn_d2t_be2': _L0_gnn_in['d2t_be2'], 'L0_gnn_t2d_w1': _L0_gnn_in['t2d_w1'], 'L0_gnn_t2d_b1': _L0_gnn_in['t2d_b1'], 'L0_gnn_t2d_g1': _L0_gnn_in['t2d_g1'], 'L0_gnn_t2d_be1': _L0_gnn_in['t2d_be1'], 'L0_gnn_t2d_w2': _L0_gnn_in['t2d_w2'], 'L0_gnn_t2d_b2': _L0_gnn_in['t2d_b2'], 'L0_gnn_t2d_g2': _L0_gnn_in['t2d_g2'], 'L0_gnn_t2d_be2': _L0_gnn_in['t2d_be2'], 'L0_gnn_node_w': _L0_gnn_in['node_w'], 'L0_gnn_node_b': _L0_gnn_in['node_b'], 'L0_gnn_node_g': _L0_gnn_in['node_g'], 'L0_gnn_node_be': _L0_gnn_in['node_be'], 'L0_gnn_self_w': _L0_gnn_in['self_w'], 'L0_gnn_self_b': _L0_gnn_in['self_b'], 'L0_gnn_self_g': _L0_gnn_in['self_g'], 'L0_gnn_self_be': _L0_gnn_in['self_be'], 'L1_gnn_wm000': _L1_gnn_in['wm000'], 'L1_gnn_wm011': _L1_gnn_in['wm011'], 'L1_gnn_wm101': _L1_gnn_in['wm101'], 'L1_gnn_wm110': _L1_gnn_in['wm110'], 'L1_gnn_lm0': _L1_gnn_in['lm0'], 'L1_gnn_lm1': _L1_gnn_in['lm1'], 'L1_gnn_wu000': _L1_gnn_in['wu000'], 'L1_gnn_wu011': _L1_gnn_in['wu011'], 'L1_gnn_wu101': _L1_gnn_in['wu101'], 'L1_gnn_wu110': _L1_gnn_in['wu110'], 'L1_gnn_lu0': _L1_gnn_in['lu0'], 'L1_gnn_lu1': _L1_gnn_in['lu1']}

def reference(x, src, dst, edge_attr_4, edge_attr_64, node_vec1, L0_gnn_w_att, L0_gnn_b_att, L0_gnn_d2t_w1, L0_gnn_d2t_b1, L0_gnn_d2t_g1, L0_gnn_d2t_be1, L0_gnn_d2t_w2, L0_gnn_d2t_b2, L0_gnn_d2t_g2, L0_gnn_d2t_be2, L0_gnn_t2d_w1, L0_gnn_t2d_b1, L0_gnn_t2d_g1, L0_gnn_t2d_be1, L0_gnn_t2d_w2, L0_gnn_t2d_b2, L0_gnn_t2d_g2, L0_gnn_t2d_be2, L0_gnn_node_w, L0_gnn_node_b, L0_gnn_node_g, L0_gnn_node_be, L0_gnn_self_w, L0_gnn_self_b, L0_gnn_self_g, L0_gnn_self_be, L1_gnn_wm000, L1_gnn_wm011, L1_gnn_wm101, L1_gnn_wm110, L1_gnn_lm0, L1_gnn_lm1, L1_gnn_wu000, L1_gnn_wu011, L1_gnn_wu101, L1_gnn_wu110, L1_gnn_lu0, L1_gnn_lu1):
    import jax
    import jax.numpy as jnp

    def _L0_gnn_ref(x, edge_index, edge_attr, w_att, b_att, d2t_w1, d2t_b1, d2t_g1, d2t_be1, d2t_w2, d2t_b2, d2t_g2, d2t_be2, t2d_w1, t2d_b1, t2d_g1, t2d_be1, t2d_w2, t2d_b2, t2d_g2, t2d_be2, node_w, node_b, node_g, node_be, self_w, self_b, self_g, self_be):
        import jax, jax.numpy as jnp
        import numpy as np
        N_NODES, N_EDGES = (6250, 50000)
        D, SPLIT, EA, H = (128, 32, 64, 256)
        IN = D + EA
        EPS = 1e-05
        SLOPE = 0.01

        def _ln(x, g, b):
            m = x.mean(-1, keepdims=True)
            v = ((x - m) ** 2).mean(-1, keepdims=True)
            return (x - m) * jax.lax.rsqrt(v + EPS) * g + b

        def _block(x, w, b, g, be):
            return jax.nn.relu(_ln(x @ w + b, g, be))

        def _masked_softmax(logits, mask):
            z = jnp.where(mask, logits, -jnp.inf)
            z = z - jnp.max(z, axis=0, keepdims=True)
            e = jnp.where(mask, jnp.exp(z), 0.0)
            return e / jnp.sum(e, axis=0, keepdims=True)

        def _forward(x, edge_index, edge_attr, w_att, b_att, d2t_w1, d2t_b1, d2t_g1, d2t_be1, d2t_w2, d2t_b2, d2t_g2, d2t_be2, t2d_w1, t2d_b1, t2d_g1, t2d_be1, t2d_w2, t2d_b2, t2d_g2, t2d_be2, node_w, node_b, node_g, node_be, self_w, self_b, self_g, self_be):
            x_split = x[:, D:]
            xn = x[:, :D]
            row, col = (edge_index[0], edge_index[1])
            n = xn.shape[0]
            concat = jnp.concatenate([xn[col], xn[row]], axis=-1)
            logits = jax.nn.leaky_relu(concat @ w_att + b_att, SLOPE)
            flow_in = jnp.concatenate([xn[col], edge_attr], axis=-1)

            def direction(mask, w1, b1, g1, be1, w2, b2, g2, be2):
                attn = _masked_softmax(logits, mask[:, None])
                h = attn * flow_in
                h = _block(h, w1, b1, g1, be1)
                h = _block(h, w2, b2, g2, be2)
                h = jnp.where(mask[:, None], h, 0.0)
                return jax.ops.segment_sum(h, row, num_segments=n)
            flow_d2t = direction(row < col, d2t_w1, d2t_b1, d2t_g1, d2t_be1, d2t_w2, d2t_b2, d2t_g2, d2t_be2)
            flow_t2d = direction(row > col, t2d_w1, t2d_b1, t2d_g1, t2d_be1, t2d_w2, t2d_b2, t2d_g2, t2d_be2)
            flow_total = jnp.concatenate([flow_t2d, flow_d2t], axis=1)
            upd = _block(flow_total, node_w, node_b, node_g, node_be)
            upd = upd + _block(xn, self_w, self_b, self_g, self_be)
            return jnp.concatenate([upd, x_split], axis=1)
        return _forward(x, edge_index, edge_attr, w_att, b_att, d2t_w1, d2t_b1, d2t_g1, d2t_be1, d2t_w2, d2t_b2, d2t_g2, d2t_be2, t2d_w1, t2d_b1, t2d_g1, t2d_be1, t2d_w2, t2d_b2, t2d_g2, t2d_be2, node_w, node_b, node_g, node_be, self_w, self_b, self_g, self_be)

    def _L1_gnn_ref(node_features, edge_index, edge_attr_tensor, node_attr_scalar_raw, wm000, wm011, wm101, wm110, lm0, lm1, wu000, wu011, wu101, wu110, lu0, lu1):
        import jax, jax.numpy as jnp
        import numpy as np
        MUL0, MUL1 = (64, 32)
        INV_SQRT3 = 1.0 / np.sqrt(3.0)

        def _split(x):
            return (x[:, :MUL0], x[:, MUL0:].reshape(x.shape[0], MUL1, 3))

        def _merge(o0, o1):
            return jnp.concatenate([o0, o1.reshape(o1.shape[0], -1)], axis=-1)

        def _tp(x0, x1, y0, y1, w000, w011, w101, w110):
            fan0 = x0.shape[1] * y0.shape[1] + x1.shape[1] * y1.shape[1]
            fan1 = x0.shape[1] * y1.shape[1] + x1.shape[1] * y0.shape[1]
            out0 = (jnp.einsum('eu,ev,uvw->ew', x0, y0, w000) + INV_SQRT3 * jnp.einsum('euk,evk,uvw->ew', x1, y1, w110)) / np.sqrt(fan0)
            out1 = (jnp.einsum('eu,evk,uvw->ewk', x0, y1, w011) + jnp.einsum('euk,ev,uvw->ewk', x1, y0, w101)) / np.sqrt(fan1)
            return (out0, out1)

        def _lin(x0, x1, w0, w1):
            return (x0 @ w0 / np.sqrt(x0.shape[1]), jnp.einsum('euk,uv->evk', x1, w1) / np.sqrt(x1.shape[1]))
        N = node_features.shape[0]
        row, col = (edge_index[0], edge_index[1])
        r_vec = edge_attr_tensor[:, :3]
        dist = edge_attr_tensor[:, 3:4]
        e0 = dist
        e1 = r_vec[:, None, :]
        xj0, xj1 = _split(node_features[col])
        m0, m1 = _tp(xj0, xj1, e0, e1, wm000, wm011, wm101, wm110)
        d0, d1 = _lin(xj0, xj1, lm0, lm1)
        msgs = _merge(m0 + d0, m1 + d1)
        agg = jax.ops.segment_sum(msgs, row, num_segments=N)
        a0, a1 = _split(agg)
        x0, x1 = _split(node_features)
        u0, u1 = _tp(x0, x1, a0, a1, wu000, wu011, wu101, wu110)
        ud0, ud1 = _lin(x0, x1, lu0, lu1)
        return node_features + _merge(u0 + ud0, u1 + ud1)
    edge_index = jnp.stack([src, dst])
    x = _layernorm(x + _L0_gnn_ref(x, edge_index, edge_attr_64, L0_gnn_w_att, L0_gnn_b_att, L0_gnn_d2t_w1, L0_gnn_d2t_b1, L0_gnn_d2t_g1, L0_gnn_d2t_be1, L0_gnn_d2t_w2, L0_gnn_d2t_b2, L0_gnn_d2t_g2, L0_gnn_d2t_be2, L0_gnn_t2d_w1, L0_gnn_t2d_b1, L0_gnn_t2d_g1, L0_gnn_t2d_be1, L0_gnn_t2d_w2, L0_gnn_t2d_b2, L0_gnn_t2d_g2, L0_gnn_t2d_be2, L0_gnn_node_w, L0_gnn_node_b, L0_gnn_node_g, L0_gnn_node_be, L0_gnn_self_w, L0_gnn_self_b, L0_gnn_self_g, L0_gnn_self_be), axis=-1)
    x = _layernorm(x + _L1_gnn_ref(x, edge_index, edge_attr_4, node_vec1, L1_gnn_wm000, L1_gnn_wm011, L1_gnn_wm101, L1_gnn_wm110, L1_gnn_lm0, L1_gnn_lm1, L1_gnn_wu000, L1_gnn_wu011, L1_gnn_wu101, L1_gnn_wu110, L1_gnn_lu0, L1_gnn_lu1), axis=-1)
    return x

_drawn_inputs = setup_inputs


def setup_inputs(seed=0):
    import zlib

    import numpy as np

    out = dict(_drawn_inputs(seed))
    spreads = {}
    factors = {'edge_attr_64': 8.0,
     'L0_gnn_w_att': 8.0,
     'L0_gnn_d2t_w1': 8.0,
     'L0_gnn_d2t_b2': 3.334,
     'L0_gnn_t2d_w1': 8.0,
     'L0_gnn_t2d_b2': 3.482,
     'L0_gnn_node_b': 8.0,
     'L0_gnn_self_b': 3.905}
    for name, (base, spread) in spreads.items():
        noise = np.random.default_rng([zlib.crc32(name.encode()), seed]).standard_normal(out[name].shape)
        drawn = base * np.exp(spread * noise) if base else spread * noise
        out[name] = jnp.asarray(drawn.astype(out[name].dtype))
    for name, factor in factors.items():
        out[name] = (out[name] * factor).astype(out[name].dtype)
    return out
```

```python
from contextlib import ExitStack

import concourse.bass as bass
from concourse import mybir

F32 = mybir.dt.float32
I32 = mybir.dt.int32
BF16 = mybir.dt.bfloat16
ALU = mybir.AluOpType
ACT = mybir.ActivationFunctionType
AX_X = mybir.AxisListType.X
RMAX = bass.bass_isa.ReduceOp.max
RADD = bass.bass_isa.ReduceOp.add

P = 128
N = 6250
NBLK = -(-N // P)
NPAD = NBLK * P
NLAST = N - (NBLK - 1) * P
E = 106250
EP = 125
ET = E // EP
D = 128
DX = 160
EA = 64
H = 256
BINS = 2 * NBLK
TPG = 2
SLOTS = TPG * P
GROUPS = (E + BINS * (SLOTS - 1)) // SLOTS
M0, M1 = 64, 32
LN_EPS = 1e-5
SLOPE = 0.01
BIG = 1e30

R_EA, R_E1, R_E0, R_ATT, R_LOC1, R_LOC0, R_COL = 0, 64, 67, 68, 69, 70, 71
RW = 72
Q_X, Q_E0, Q_E1, Q_Z = 0, DX, 2 * DX, 2 * DX + 3 * M0
QW = Q_Z + M1

RING = 4
AHEAD = 8


class Step:

    def __init__(self, trip, unroll, at):
        self.trip, self.unroll, self.at = trip, unroll, at

    def back(self, lag):
        return Step(self.trip, self.unroll, self.at - lag)

    def n(self, per=1, plus=0):
        if self.trip is None:
            return self.at * per + plus
        return self.trip * (self.unroll * per) + (self.at * per + plus)

    def turn(self, ring, per=1, plus=0):
        if self.trip is None:
            return self.at // ring * per + plus
        return self.trip * (self.unroll // ring * per) + (self.at // ring * per + plus)

    def slot(self, ring):
        return self.at % ring


def pipeline(eng, total, unroll, stages):
    most = max(lag for lag, _ in stages)
    lead = -(-(most + unroll) // unroll) * unroll
    trips = (total - lead) // unroll

    def body(step):
        for lag, stage in stages:
            if step.trip is not None or 0 <= step.at - lag < total:
                stage(step.back(lag))

    for at in range(lead):
        body(Step(None, unroll, at))
    with eng.Fori(0, trips) as trip:
        for u in range(unroll):
            body(Step(trip, unroll, lead + u))
    for at in range(lead + trips * unroll, total + most):
        body(Step(None, unroll, at))


class Waits:

    def __init__(self, eng, woken):
        self.eng, self.woken = eng, woken

    def __call__(self, sem, count):
        if isinstance(count, int):
            if count > 0:
                self.eng.wait_ge(sem, count)
        else:
            self.eng.wait_ge(sem, count)
            self.eng.sem_inc(self.woken, 1)


def split(rows):
    cut = rows // 16 * 16
    return [(0, cut), (cut, rows)]


def build(nc, t, out):
    with ExitStack() as ctx:
        ctx.enter_context(nc.allow_non_contiguous_dma(reason="small weights and tables"))

        def sb(name, shape, dt=F32, into=ctx):
            return into.enter_context(nc.sbuf_tensor(name, shape, dt))

        def sem(name):
            return ctx.enter_context(nc.semaphore(name))

        woken = {e: sem(f"woken_{e}") for e in ("sp", "act", "dve", "pe", "pool")}
        dram = {
            "u": nc.dram_tensor("u_table", (2 * NPAD, H), F32).ap(),
            "x1": nc.dram_tensor("x1_table", (2 * NPAD, DX), F32).ap(),
            "a": nc.dram_tensor("a_table", (NPAD, 1), F32).ap(),
            "b": nc.dram_tensor("b_table", (NPAD, 1), F32).ap(),
            "rec": nc.dram_tensor("records", (GROUPS * SLOTS, RW), F32).ap(),
            "tab": nc.dram_tensor("group_table", (3, GROUPS), I32).ap(),
            "mix": nc.dram_tensor("mix_weights", (QW + DX, DX), F32).ap(),
        }
        x_s = sb("x_s", [P, NBLK, DX])
        ident = sb("ident", [P, P])
        iota_f = sb("iota_f", [P, P])
        eps_s = sb("eps_s", [P, 1])
        zero_s = sb("zero_s", [P, 1])
        tab_s = sb("tab_s", [1, 3, GROUPS], I32)
        kit = (nc, t, out, dram, woken, x_s, ident, iota_f, eps_s, zero_s, tab_s)
        rec_in = [sem(f"rec_in{i}") for i in range(AHEAD)]
        rows_in = [sem(f"rows_in{i}") for i in range(AHEAD)]
        with ExitStack() as c:
            first = lay_first_weights(nc, c)
            phase_node_tables(kit, first)
            phase_sort(kit)
            with ExitStack() as c2:
                acc = c2.enter_context(nc.sbuf_tensor("flow_sum", [P, BINS, D], F32))
                phase_first_edges(kit, first, acc, rec_in, rows_in)
                phase_first_nodes(kit, first, acc)
        with ExitStack() as c:
            acc = c.enter_context(nc.sbuf_tensor("mix_sum", [P, NBLK, QW], F32))
            phase_second_edges(kit, acc, rec_in, rows_in)
            phase_second_nodes(kit, acc)


ROWS = ["d2t_b2", "t2d_b2", "d2t_g2", "t2d_g2", "d2t_be2", "t2d_be2", "node_b", "self_b", "node_g", "self_g",
        "node_be", "self_be"]
B2, G2, BE2, NSB, NSG, NSBE = 0, 2, 4, 6, 8, 10


def lay_first_weights(nc, ctx):
    def sb(name, shape):
        return ctx.enter_context(nc.sbuf_tensor(name, shape, F32))

    return {
        "w1x": sb("w1x", [P, 2, H]),
        "w1e": sb("w1e", [EA + 1, 2, H]),
        "w2": sb("w2", [P, 2, 2, D]),
        "gb1": sb("gb1", [P, 2, 4]),
        "rows": sb("rows", [P, 12, D]),
        "nsw": sb("nsw", [P, 3, D]),
        "watt": sb("watt", [P, 2]),
        "batt": sb("batt", [P, 1]),
    }


def phase_node_tables(kit, w):
    nc, t, out, dram, woken, x_s, ident, iota_f, eps_s, zero_s, tab_s = kit
    with ExitStack() as ctx:
        def sb(name, shape, dt=F32):
            return ctx.enter_context(nc.sbuf_tensor("a_" + name, shape, dt))

        def ps(name, shape):
            return ctx.enter_context(nc.psum_tensor("a_" + name, shape, F32))

        def sem(name):
            return ctx.enter_context(nc.semaphore(name))

        pad_rec = sb("pad_rec", [P, 16, RW])
        means = sb("means", [P, 32])
        xc = sb("xc", [P, 4, D])
        xt = sb("xt", [P, 4, D])
        u_out = sb("u_out", [P, 4, 2 * H])
        ab_s = sb("ab_s", [P, NBLK, 2])
        p_t = [ps(f"p_t{i}", [P, 512]) for i in range(2)]
        p_u = [ps(f"p_u{i}", [P, 512]) for i in range(2)]
        p_ab = [ps(f"p_ab{i}", [P, 512]) for i in range(2)]
        loaded, cleared, constants = sem("a_loaded"), sem("a_cleared"), sem("a_constants")
        dve_chain, pool_chain, centred = sem("a_dve_chain"), sem("a_pool_chain"), sem("a_centred")
        x_staged, x_turned, xt_ready = sem("a_x_staged"), sem("a_x_turned"), sem("a_xt_ready")
        u_made, u_ready = sem("a_u_made"), sem("a_u_ready")
        u_stored = [sem(f"a_u_stored{i}") for i in range(4)]
        stored = sem("a_stored")
        loads = []

        def load(dst, src):
            loads.append((dst, src))

        load(x_s[:, 0:NBLK - 1, :], t["x"][0:(NBLK - 1) * P, :].rearrange("(b p) f -> p b f", p=P))
        load(x_s[0:NLAST, NBLK - 1, :], t["x"][(NBLK - 1) * P:N, :])
        for d, pre in enumerate(("L0_gnn_d2t_", "L0_gnn_t2d_")):
            load(w["w1x"][:, d, :], t[pre + "w1"][0:D, :])
            load(w["w1e"][0:EA, d, :], t[pre + "w1"][D:D + EA, :])
            load(w["w1e"][EA:EA + 1, d, :], t[pre + "b1"].unsqueeze(0))
            load(w["w2"][:, d, :, :], t[pre + "w2"].rearrange("(c k) f -> k c f", c=2))
            load(w["gb1"][:, d, 0:2], t[pre + "g1"].rearrange("(c k) -> k c", c=2))
            load(w["gb1"][:, d, 2:4], t[pre + "be1"].rearrange("(c k) -> k c", c=2))
        for i, name in enumerate(ROWS):
            load(w["rows"][:, i, :], t["L0_gnn_" + name].partition_broadcast(P))
        load(w["nsw"][:, 0:2, :], t["L0_gnn_node_w"].rearrange("(c k) f -> k c f", c=2))
        load(w["nsw"][:, 2, :], t["L0_gnn_self_w"])
        load(w["watt"][:, :], t["L0_gnn_w_att"].rearrange("(c k) o -> k (c o)", c=2))
        load(w["batt"][:, :], t["L0_gnn_b_att"].partition_broadcast(P))

        block = ctx.enter_context(nc.Block())

        @block.sync
        def _(sp):
            wait = Waits(sp, woken["sp"])
            wait(cleared, 2)
            for dst, src in loads:
                sp.dma_start(dst, src).then_inc(loaded, 16)
            sp.dma_start(dram["rec"].rearrange("(p q r) w -> p q (r w)", p=P, r=16),
                         pad_rec[:, :, :].rearrange("p r w -> p (r w)").unsqueeze(1)
                         .to_broadcast([P, GROUPS * SLOTS // (16 * P), 16 * RW])).then_inc(stored, 16)

            def store(s):
                r = s.slot(4)
                wait(u_ready, s.n(1, 1))
                sp.dma_start(dram["u"].rearrange("(d n) f -> n d f", d=2)[bass.ds(s.n(P), P), :, :],
                             u_out[:, r, :].rearrange("p (d f) -> p d f", d=2)).then_inc(u_stored[r], 16)

            pipeline(sp, NBLK, 4, [(0, store)])
            for i in range(2):
                sp.dma_start((dram["a"], dram["b"])[i].rearrange("(b p) o -> p (b o)", p=P),
                             ab_s[:, :, i]).then_inc(stored, 16)
            wait(stored, 48)
            for r in range(4):
                wait(u_stored[r], 16 * len(range(r, NBLK, 4)))

        @block.gpsimd
        def _(pool):
            nc.gpsimd.memset(ident[:, :], 0.0).then_inc(pool_chain, 1)
            pool.wait_ge(pool_chain, 1)
            nc.gpsimd.affine_select(out=ident[:, :], in_=ident[:, :], compare_op=ALU.not_equal, fill=1.0, base=0,
                                    pattern=[[-1, P]], channel_multiplier=1).then_inc(constants, 1)
            nc.gpsimd.iota(iota_f[:, :], [[1, P]], base=0, channel_multiplier=0,
                           allow_small_or_imprecise_dtypes=True).then_inc(constants, 1)

        @block.vector
        def _(dve):
            wait = Waits(dve, woken["dve"])
            count = [0]

            def link(ins):
                count[0] += 1
                ins.then_inc(dve_chain, 1)
                dve.wait_ge(dve_chain, count[0])

            nc.vector.memset(x_s[:, NBLK - 1, :], 0.0).then_inc(cleared, 1)
            link(nc.vector.memset(pad_rec[:, :, :], 0.0))
            nc.vector.memset(pad_rec[:, :, R_LOC1:R_LOC0 + 1], -1.0).then_inc(cleared, 1)
            nc.vector.memset(zero_s[:, :], 0.0).then_inc(constants, 1)
            nc.vector.memset(eps_s[:, :], LN_EPS).then_inc(constants, 1)
            dve.wait_ge(loaded, 16 * len(loads))
            centre = [(w["w1x"][:, d, :], P, H) for d in range(2)]
            centre += [(w["w1e"][:, d, :], EA + 1, H) for d in range(2)]
            centre += [(w["w2"][:, d, c, :], P, D) for d in range(2) for c in range(2)]
            centre += [(w["rows"][:, i, :], P, D) for i in (B2, B2 + 1, NSB, NSB + 1)]
            centre += [(w["nsw"][:, i, :], P, D) for i in range(3)]
            for i, (ap, rows, width) in enumerate(centre):
                last = nc.vector.reduce_sum(means[0:rows, i:i + 1], ap, axis=AX_X)
            link(last)
            for i, (ap, rows, width) in enumerate(centre):
                last = nc.vector.tensor_scalar(means[0:rows, i:i + 1], means[0:rows, i:i + 1], -1.0 / width, None,
                                               ALU.mult)
            link(last)
            for i, (ap, rows, width) in enumerate(centre):
                last = nc.vector.tensor_scalar(ap, ap, means[0:rows, i:i + 1], None, ALU.add)
            last.then_inc(centred, 1)

            def evacuate(s):
                r, h = s.slot(4), s.slot(2)
                wait(u_made, s.n(1, 1))
                wait(u_stored[r], s.turn(4, 16))
                nc.vector.tensor_copy(ab_s[:, bass.ds(s.n(), 1), :], p_ab[h][:, 0:2].unsqueeze(1))
                nc.vector.tensor_copy(u_out[:, r, :], p_u[h][:, :]).then_inc(u_ready, 1)

            pipeline(dve, NBLK, 4, [(0, evacuate)])

        @block.scalar
        def _(act):
            wait = Waits(act, woken["act"])
            act.wait_ge(loaded, 16 * len(loads))

            def stage_x(s):
                if s.trip is not None or s.at >= 4:
                    wait(x_turned, s.n(1, -3))
                nc.scalar.copy(xc[:, s.slot(4), :].unsqueeze(1),
                               x_s[:, bass.ds(s.n(), 1), 0:D]).then_inc(x_staged, 1)

            def copy_xt(s):
                wait(x_turned, s.n(1, 1))
                if s.trip is not None or s.at >= 4:
                    wait(u_made, s.n(1, -3))
                nc.scalar.copy(xt[:, s.slot(4), :], p_t[s.slot(2)][:, 0:P]).then_inc(xt_ready, 1)

            pipeline(act, NBLK, 4, [(1, copy_xt), (0, stage_x)])

        @block.tensor
        def _(pe):
            wait = Waits(pe, woken["pe"])
            pe.wait_ge(constants, 4)
            pe.wait_ge(centred, 1)

            def turn(s):
                wait(x_staged, s.n(1, 1))
                if s.trip is not None or s.at >= 2:
                    wait(xt_ready, s.n(1, -1))
                nc.tensor.transpose(p_t[s.slot(2)][:, 0:P], xc[:, s.slot(4), :], ident[:, :]).then_inc(x_turned, 1)

            def product(s):
                h = s.slot(2)
                wait(xt_ready, s.n(1, 1))
                if s.trip is not None or s.at >= 2:
                    wait(u_ready, s.n(1, -1))
                xtb = xt[:, s.slot(4), :]
                nc.tensor.matmul(p_ab[h][:, 0:2], xtb, w["watt"][:, :], start=True, stop=True)
                nc.tensor.matmul(p_u[h][:, :], xtb, w["w1x"][:, :, :].rearrange("p d f -> p (d f)"), start=True,
                                 stop=True).then_inc(u_made, 1)

            pipeline(pe, NBLK, 4, [(1, product), (0, turn)])


def phase_sort(kit):
    nc, t, out, dram, woken, x_s, ident, iota_f, eps_s, zero_s, tab_s = kit
    LOT = 5
    LOTS = ET // LOT
    with ExitStack() as ctx:
        def sb(name, shape, dt=F32):
            return ctx.enter_context(nc.sbuf_tensor("b_" + name, shape, dt))

        def ps(name, shape):
            return ctx.enter_context(nc.psum_tensor("b_" + name, shape, F32))

        def sem(name):
            return ctx.enter_context(nc.semaphore(name))

        row_i, col_i = sb("row_i", [EP, ET], I32), sb("col_i", [EP, ET], I32)
        blk_i, loc_i = sb("blk_i", [EP, ET], I32), sb("loc_i", [EP, ET], I32)
        row_f, col_f = sb("row_f", [EP, ET]), sb("col_f", [EP, ET])
        up, down = sb("up", [EP, ET]), sb("down", [EP, ET])
        bin_f = sb("bin_f", [EP, ET])
        tail = sb("tail", [EP, ET, RW - EA])
        ea4_s = sb("ea4_s", [EP, ET, 4])
        from_col, from_row = sb("from_col", [EP, ET]), sb("from_row", [EP, ET])
        slot_f, slot_i = sb("slot_f", [EP, ET]), sb("slot_i", [EP, ET], I32)
        tmp = sb("tmp", [EP, 2, ET])
        lim = sb("lim", [EP, 2, ET])
        junk = sb("junk", [P, 2, ET], BF16)
        count_s = sb("count_s", [EP, BINS])
        held = sb("held", [EP, 2, BINS])
        junk2 = sb("junk2", [EP, 2, BINS])
        lower = sb("lower", [EP, EP])
        ones = sb("ones", [P, P])
        size_i, size_f = sb("size_i", [P, BINS], I32), sb("size_f", [P, BINS])
        ends, starts = sb("ends", [P, BINS]), sb("starts", [P, BINS])
        gstart = sb("gstart", [P, GROUPS // P])
        tab_f = sb("tab_f", [P, 3, GROUPS // P])
        tab_i = sb("tab_i", [P, 3, GROUPS // P], I32)
        stats = sb("stats", [P, 8])
        batt = sb("batt_s", [EP, 1])
        icol, irow = sb("icol", [EP, 2, LOT], I32), sb("irow", [EP, 2, LOT], I32)
        gcol, grow = sb("gcol", [EP, 2, LOT]), sb("grow", [EP, 2, LOT])
        stage = sb("stage", [EP, 4, LOT, RW])
        islot = sb("islot", [EP, 4, LOT], I32)
        p_low, p_all = ps("p_low", [P, 512]), ps("p_all", [P, 512])

        loaded, ready = sem("b_loaded"), sem("b_ready")
        dve_chain, pool_chain = sem("b_dve_chain"), sem("b_pool_chain")
        i_staged = sem("b_i_staged")
        gathered = [sem(f"b_gathered{i}") for i in range(2)]
        logits_in = sem("b_logits_in")
        hist_done, hist_summed = sem("b_hist_done"), sem("b_hist_summed")
        held_step, hist_step = sem("b_held_step"), sem("b_hist_step")
        tab_ready, tab_out, tab_in = sem("b_tab_ready"), sem("b_tab_out"), sem("b_tab_in")
        max_part, max_all, exp_done = sem("b_max_part"), sem("b_max_all"), sem("b_exp_done")
        sum_all, tail_ready = sem("b_sum_all"), sem("b_tail_ready")
        max_negated = sem("b_max_negated")

        with nc.Block() as block:
            @block.sync
            def _(sp):
                wait = Waits(sp, woken["sp"])
                for lo, hi in split(EP):
                    for dst, src in ((row_i, t["src"]), (col_i, t["dst"])):
                        sp.dma_start(dst[lo:hi, :], src.rearrange("(p t) -> p t", p=EP)[lo:hi, :]).then_inc(loaded, 16)
                for lo, hi in split(EP):
                    sp.dma_start(ea4_s[lo:hi, :, :], t["edge_attr_4"].rearrange("(p t) w -> p t w", p=EP)[lo:hi, :, :])\
                        .then_inc(loaded, 16)
                sp.dma_start(batt[:, :], t["L0_gnn_b_att"].partition_broadcast(EP)).then_inc(loaded, 16)
                wait(tab_ready, 1)
                sp.dma_start(dram["tab"].rearrange("c (s p) -> p c s", p=P), tab_i[:, :, :]).then_inc(tab_out, 16)
                wait(tab_out, 16)
                sp.dma_start(tab_s[:, :, :], dram["tab"].unsqueeze(0)).then_inc(tab_in, 16)
                wait(tab_in, 16)

            @block.gpsimd
            def _(pool):
                wait = Waits(pool, woken["pool"])
                nc.gpsimd.memset(lower[:, :], 1.0).then_inc(pool_chain, 1)
                pool.wait_ge(pool_chain, 1)
                nc.gpsimd.affine_select(out=lower[:, :], in_=lower[:, :], compare_op=ALU.is_gt, fill=0.0, base=0,
                                        pattern=[[1, EP]], channel_multiplier=-1).then_inc(ready, 1)
                nc.gpsimd.iota(gstart[:, :], [[P, GROUPS // P]], base=0, channel_multiplier=1,
                               allow_small_or_imprecise_dtypes=True).then_inc(ready, 1)

                def gather(s):
                    h = s.slot(2)
                    wait(i_staged, s.n(1, 1))
                    for j in range(LOT):
                        for table, index, dst in ((dram["a"], icol, gcol), (dram["b"], irow, grow)):
                            nc.gpsimd.indirect_dma_start(
                                dst[:, h, j:j + 1], None, table,
                                bass.IndirectOffsetOnAxis(ap=index[:, h, j:j + 1], axis=0)).then_inc(gathered[h], 16)

                pipeline(pool, LOTS, 2, [(0, gather)])
                pool.wait_ge(max_part, 1)
                nc.gpsimd.partition_all_reduce(stats[:, 2:4], stats[:, 0:2], P, RMAX).then_inc(max_all, 1)
                pool.wait_ge(exp_done, 2)
                nc.gpsimd.partition_all_reduce(stats[:, 6:8], stats[:, 4:6], P, RADD).then_inc(sum_all, 1)

            @block.scalar
            def _(act):
                wait = Waits(act, woken["act"])
                act.wait_ge(loaded, 16 * 7)

                def take(s):
                    h = s.slot(2)
                    wait(gathered[h], s.turn(2, 32 * LOT, 32 * LOT))
                    nc.scalar.copy(from_col[:, bass.ds(s.n(LOT), LOT)], gcol[:, h, :]).then_inc(logits_in, 1)
                    nc.scalar.copy(from_row[:, bass.ds(s.n(LOT), LOT)], grow[:, h, :]).then_inc(logits_in, 1)

                def give(s):
                    h = s.slot(2)
                    if s.trip is not None or s.at >= 2:
                        wait(logits_in, s.n(2, -2))
                    nc.scalar.copy(icol[:, h, :], col_i[:, bass.ds(s.n(LOT), LOT)])
                    nc.scalar.copy(irow[:, h, :], row_i[:, bass.ds(s.n(LOT), LOT)]).then_inc(i_staged, 1)

                pipeline(act, LOTS, 2, [(2, take), (0, give)])
                act.wait_ge(max_negated, 1)
                for d in range(2):
                    nc.scalar.activation(tmp[:, d, :], lim[:, d, :], ACT.Exp, bias=stats[0:EP, 2 + d:3 + d],
                                         accum_out=stats[0:EP, 4 + d:5 + d]).then_inc(exp_done, 1)

            @block.tensor
            def _(pe):
                pe.wait_ge(ready, 3)
                pe.wait_ge(hist_done, 1)
                nc.tensor.matmul(p_low[0:EP, 0:BINS], lower[:, :], count_s[:, :], start=True, stop=True)
                nc.tensor.matmul(p_all[:, 0:BINS], ones[0:EP, :], count_s[:, :], start=True, stop=True)\
                    .then_inc(hist_summed, 1)

            @block.vector
            def _(dve):
                wait = Waits(dve, woken["dve"])
                count = [0]

                def link(ins):
                    count[0] += 1
                    ins.then_inc(dve_chain, 1)
                    dve.wait_ge(dve_chain, count[0])

                V = nc.vector
                V.memset(ones[:, :], 1.0).then_inc(ready, 1)
                V.memset(stats[:, 0:2], -BIG)
                link(V.memset(stats[:, 4:6], 0.0))
                dve.wait_ge(loaded, 16 * 7)
                V.tensor_copy(row_f[:, :], row_i[:, :])
                V.tensor_copy(col_f[:, :], col_i[:, :])
                V.tensor_single_scalar(blk_i[:, :], row_i[:, :], 7, ALU.logical_shift_right)
                link(V.tensor_single_scalar(loc_i[:, :], row_i[:, :], P - 1, ALU.bitwise_and))
                V.tensor_copy(bin_f[:, :], blk_i[:, :])
                V.tensor_copy(tail[:, :, R_LOC1 - EA], loc_i[:, :])
                V.tensor_tensor(up[:, :], row_f[:, :], col_f[:, :], ALU.is_lt)
                V.tensor_tensor(down[:, :], row_f[:, :], col_f[:, :], ALU.is_gt)
                link(V.tensor_copy(tail[:, :, 0:4], ea4_s[:, :, :]))
                V.scalar_tensor_tensor(out=bin_f[:, :], in0=down[:, :], scalar=float(NBLK), in1=bin_f[:, :],
                                       op0=ALU.mult, op1=ALU.add)
                V.scalar_tensor_tensor(out=tail[:, :, R_COL - EA], in0=down[:, :], scalar=float(NPAD),
                                       in1=col_f[:, :], op0=ALU.mult, op1=ALU.add)
                link(V.tensor_tensor(tmp[:, 0, :], up[:, :], down[:, :], ALU.add))
                link(V.scalar_tensor_tensor(out=tmp[:, 1, :], in0=tail[:, :, R_LOC1 - EA], scalar=1.0,
                                            in1=tmp[:, 0, :], op0=ALU.add, op1=ALU.mult))
                link(V.tensor_scalar(tail[:, :, R_LOC0 - EA], tmp[:, 1, :], -1.0, None, ALU.add))
                def count_bin(s):
                    if s.trip is not None or s.at >= 2:
                        wait(hist_step, s.n(1, -1))
                    V.tensor_scalar(junk[0:EP, s.slot(2), :], bin_f[:, :], iota_f[0:EP, bass.ds(s.n(), 1)], None,
                                    ALU.is_equal, ALU.add, accum_out=count_s[:, bass.ds(s.n(), 1)])\
                        .then_inc(hist_step, 1)

                pipeline(dve, BINS, 2, [(0, count_bin)])
                dve.wait_ge(hist_step, BINS)
                V.memset(junk2[:, :, :], 0.0).then_inc(hist_done, 1)
                dve.wait_ge(hist_summed, 1)
                link(V.tensor_scalar(size_i[:, :], p_all[:, 0:BINS], float(SLOTS - 1), None, ALU.add))
                link(V.tensor_scalar(size_i[:, :], size_i[:, :], 8, 8, ALU.logical_shift_right,
                                     ALU.logical_shift_left))
                link(V.tensor_copy(size_f[:, :], size_i[:, :]))
                link(V.tensor_tensor_scan(ends[:, :], ones[:, 0:BINS], size_f[:, :], 0.0, ALU.mult, ALU.add))
                link(V.tensor_tensor(starts[:, :], ends[:, :], size_f[:, :], ALU.subtract))
                V.tensor_tensor(held[:, 0, :], starts[0:EP, :], p_low[0:EP, 0:BINS], ALU.add).then_inc(held_step, 1)
                link(V.tensor_scalar(gstart[:, :], gstart[:, :], float(SLOTS), None, ALU.mult))
                for s in range(GROUPS // P):
                    last = V.tensor_scalar(junk[:, 0, BINS * s:BINS * (s + 1)], ends[:, :], gstart[:, s:s + 1], None, ALU.is_le, ALU.add,
                                           accum_out=tab_f[:, 0, s:s + 1])
                link(last)
                link(V.tensor_scalar(tab_f[:, 0, :], tab_f[:, 0, :], float(BINS - 1), None, ALU.min))
                link(V.tensor_scalar(tab_f[:, 1, :], tab_f[:, 0, :], float(NBLK), None, ALU.is_ge))
                link(V.scalar_tensor_tensor(out=tab_f[:, 2, :], in0=tab_f[:, 1, :], scalar=-float(NBLK),
                                            in1=tab_f[:, 0, :], op0=ALU.mult, op1=ALU.add))
                V.tensor_copy(tab_i[:, :, :], tab_f[:, :, :]).then_inc(tab_ready, 1)

                def place(s):
                    h = s.slot(2)
                    wait(held_step, s.n(1, 1))
                    V.scalar_tensor_tensor(out=junk2[:, h, :], in0=iota_f[0:EP, 0:BINS],
                                           scalar=bin_f[:, bass.ds(s.n(), 1)], in1=held[:, h, :],
                                           op0=ALU.is_equal, op1=ALU.mult, accum_out=slot_f[:, bass.ds(s.n(), 1)])
                    V.scalar_tensor_tensor(out=held[:, 1 - h, :], in0=iota_f[0:EP, 0:BINS],
                                           scalar=bin_f[:, bass.ds(s.n(), 1)], in1=held[:, h, :],
                                           op0=ALU.is_equal, op1=ALU.add).then_inc(held_step, 1)

                pipeline(dve, ET, 10, [(0, place)])
                dve.wait_ge(held_step, ET + 1)
                V.tensor_copy(slot_i[:, :], slot_f[:, :])
                dve.wait_ge(logits_in, 2 * LOTS)
                link(V.tensor_tensor(from_col[:, :], from_col[:, :], from_row[:, :], ALU.add))
                link(V.tensor_scalar(from_col[:, :], from_col[:, :], batt[:, :], None, ALU.add))
                link(V.scalar_tensor_tensor(out=from_row[:, :], in0=from_col[:, :], scalar=SLOPE, in1=from_col[:, :],
                                            op0=ALU.mult, op1=ALU.max))
                V.tensor_scalar(lim[:, 0, :], up[:, :], 2 * BIG, -BIG, ALU.mult, ALU.add)
                link(V.tensor_scalar(lim[:, 1, :], down[:, :], 2 * BIG, -BIG, ALU.mult, ALU.add))
                for d in range(2):
                    last = V.tensor_tensor(lim[:, d, :], lim[:, d, :], from_row[:, :], ALU.min)
                link(last)
                for d in range(2):
                    last = V.reduce_max(stats[0:EP, d:d + 1], lim[:, d, :], axis=AX_X)
                last.then_inc(max_part, 1)
                dve.wait_ge(max_all, 1)
                V.tensor_scalar(stats[:, 2:4], stats[:, 2:4], -1.0, None, ALU.mult).then_inc(max_negated, 1)
                dve.wait_ge(exp_done, 2)
                V.tensor_tensor(tmp[:, 0, :], tmp[:, 0, :], up[:, :], ALU.mult)
                V.tensor_tensor(tmp[:, 1, :], tmp[:, 1, :], down[:, :], ALU.mult)
                dve.wait_ge(sum_all, 1)
                link(V.reciprocal(stats[:, 6:8], stats[:, 6:8]))
                link(V.tensor_scalar(tmp[:, 0, :], tmp[:, 0, :], stats[0:EP, 6:7], None, ALU.mult))
                V.scalar_tensor_tensor(out=tail[:, :, R_ATT - EA], in0=tmp[:, 1, :], scalar=stats[0:EP, 7:8],
                                       in1=tmp[:, 0, :], op0=ALU.mult, op1=ALU.add).then_inc(tail_ready, 1)

        features_in = [sem(f"s_features_in{i}") for i in range(4)]
        staged = sem("s_staged")
        scattered = [sem(f"s_scattered{i}") for i in range(4)]
        with nc.Block() as block:
            @block.sync
            def _(sp):
                wait = Waits(sp, woken["sp"])

                def features(s):
                    r = s.slot(4)
                    wait(scattered[r], s.turn(4, 16 * LOT))
                    for lo, hi in split(EP):
                        sp.dma_start(stage[lo:hi, r, :, 0:EA],
                                     t["edge_attr_64"].rearrange("(p t) w -> p t w", p=EP)
                                     [lo:hi, bass.ds(s.n(LOT), LOT), :]).then_inc(features_in[r], 16)

                pipeline(sp, LOTS, 4, [(0, features)])

            @block.vector
            def _(dve):
                wait = Waits(dve, woken["dve"])

                def tails(s):
                    r = s.slot(4)
                    wait(scattered[r], s.turn(4, 16 * LOT))
                    nc.vector.tensor_copy(stage[:, r, :, EA:RW], tail[:, bass.ds(s.n(LOT), LOT), :])
                    nc.vector.tensor_copy(islot[:, r, :], slot_i[:, bass.ds(s.n(LOT), LOT)]).then_inc(staged, 1)

                pipeline(dve, LOTS, 4, [(0, tails)])

            @block.gpsimd
            def _(pool):
                wait = Waits(pool, woken["pool"])

                def scatter(s):
                    r = s.slot(4)
                    wait(staged, s.n(1, 1))
                    wait(features_in[r], s.turn(4, 32, 32))
                    for j in range(LOT):
                        nc.gpsimd.indirect_dma_start(
                            dram["rec"], bass.IndirectOffsetOnAxis(ap=islot[:, r, j:j + 1], axis=0),
                            stage[:, r, j, :], None).then_inc(scattered[r], 16)

                pipeline(pool, LOTS, 4, [(0, scatter)])
                for r in range(4):
                    wait(scattered[r], 16 * LOT * len(range(r, LOTS, 4)))


def phase_first_edges(kit, w, acc, rec_in, u_in):
    nc, t, out, dram, woken, x_s, ident, iota_f, eps_s, zero_s, tab_s = kit
    T = TPG
    with ExitStack() as ctx:
        def sb(name, shape, dt=F32):
            return ctx.enter_context(nc.sbuf_tensor("e_" + name, shape, dt))

        def ps(name):
            return ctx.enter_context(nc.psum_tensor("e_" + name, [P, 512], F32))

        def sem(name):
            return ctx.enter_context(nc.semaphore(name))

        rec = sb("rec", [P, AHEAD, T, RW])
        index = sb("index", [P, AHEAD, T], I32)
        ea1 = sb("ea1", [P, RING, T, EA + 1])
        ea1_t = sb("ea1_t", [EA + 1, RING, T * P])
        u = sb("u", [P, AHEAD, T, H])
        v = sb("v", [P, RING, T, H])
        vn = sb("vn", [P, RING, T, H])
        h_t = sb("h_t", [P, RING, 2, T * P])
        v2 = sb("v2", [P, RING, T, D])
        h2 = sb("h2", [P, RING, T, D])
        onehot = sb("onehot", [P, AHEAD, T, P])
        junk = sb("junk", [P, RING, 2, T, H])
        sq, dev, inv = sb("sq", [P, RING, 2, T]), sb("dev", [P, RING, 2, T]), sb("inv", [P, RING, 2, T])
        p_ea = [ps(f"p_ea{i}") for i in range(2)]
        p_v = [ps(f"p_v{i}") for i in range(2)]
        p_turn = [ps(f"p_turn{i}") for i in range(2)]
        p_v2, p_sum = ps("p_v2"), ps("p_sum")

        rec_used, index_ready, ea1_ready = sem("e_rec_used"), sem("e_index_ready"), sem("e_ea1_ready")
        ea1_turned, ea1t_ready, v_in_psum = sem("e_ea1_turned"), sem("e_ea1t_ready"), sem("e_v_in_psum")
        v_ready, sq1_done, dev1_ready = sem("e_v_ready"), sem("e_sq1_done"), sem("e_dev1_ready")
        inv1_done, vn_ready, v_turned = sem("e_inv1_done"), sem("e_vn_ready"), sem("e_v_turned")
        ht_ready, v2_in_psum, v2_ready = sem("e_ht_ready"), sem("e_v2_in_psum"), sem("e_v2_ready")
        sq2_done, dev2_ready, norm2 = sem("e_sq2_done"), sem("e_dev2_ready"), sem("e_norm2")
        h2_ready, summed, added = sem("e_h2_ready"), sem("e_summed"), sem("e_added")
        cleared = sem("e_cleared")
        block = ctx.enter_context(nc.Block())

        @block.sync
        def _(sp):
            wait = Waits(sp, woken["sp"])

            def load(s):
                r = s.slot(AHEAD)
                wait(rec_used, s.n(1, 1 - AHEAD))
                sp.dma_start(rec[:, r, :, :].rearrange("p t w -> p (t w)"),
                             dram["rec"].rearrange("(g p t) w -> g p (t w)", p=P, t=T)[bass.ds(s.n(), 1), :, :]
                             .rearrange("g p w -> (g p) w")).then_inc(rec_in[r], 16)

            pipeline(sp, GROUPS, AHEAD, [(0, load)])

        @block.gpsimd
        def _(pool):
            wait = Waits(pool, woken["pool"])

            def gather(s):
                r = s.slot(AHEAD)
                wait(index_ready, s.n(1, 1))
                for j in range(T):
                    nc.gpsimd.indirect_dma_start(
                        u[:, r, j, :], None, dram["u"],
                        bass.IndirectOffsetOnAxis(ap=index[:, r, j:j + 1], axis=0)).then_inc(u_in[r], 16)

            pipeline(pool, GROUPS, AHEAD, [(0, gather)])

        @block.tensor
        def _(pe):
            wait = Waits(pe, woken["pe"])
            pe.wait_ge(cleared, 2)

            def turn_ea(s):
                r = s.slot(RING)
                wait(ea1_ready, s.n(1, 1))
                for j in range(T):
                    last = nc.tensor.transpose(p_ea[s.slot(2)][0:EA + 1, j * P:(j + 1) * P], ea1[:, r, j, :],
                                               ident[:, :])
                last.then_inc(ea1_turned, 1)

            def first_product(s):
                r, h = s.slot(RING), s.slot(2)
                d = pe.value_load(tab_s[0:1, 1, bass.ds(s.n(), 1)], min_val=0, max_val=1)
                wait(ea1t_ready, s.n(1, 1))
                if s.trip is not None or s.at >= 2:
                    wait(v_ready, s.n(1, -1))
                for j in range(T):
                    last = nc.tensor.matmul(p_v[h][:, j * H:(j + 1) * H], ea1_t[:, r, j * P:(j + 1) * P],
                                            w["w1e"][:, :, :].rearrange("p d f -> p (d f)")[:, bass.ds(d * H, H)],
                                            start=True, stop=True)
                last.then_inc(v_in_psum, 1)

            def turn_v(s):
                r, h = s.slot(RING), s.slot(2)
                wait(vn_ready, s.n(1, 1))
                for c in range(2):
                    for j in range(T):
                        last = nc.tensor.transpose(p_turn[h][:, (c * T + j) * P:(c * T + j + 1) * P],
                                                   vn[:, r, j, c * P:(c + 1) * P], ident[:, :])
                last.then_inc(v_turned, 1)

            def second_product(s):
                r, h = s.slot(RING), s.slot(2)
                d = pe.value_load(tab_s[0:1, 1, bass.ds(s.n(), 1)], min_val=0, max_val=1)
                wait(ht_ready, s.n(1, 1))
                if s.trip is not None or s.at >= 1:
                    wait(v2_ready, s.n())
                w2 = w["w2"][:, :, :, :].rearrange("p d c f -> p (d c f)")
                for j in range(T):
                    for c in range(2):
                        last = nc.tensor.matmul(p_v2[:, (h * T + j) * D:(h * T + j + 1) * D],
                                                h_t[:, r, c, j * P:(j + 1) * P], w2[:, bass.ds(d * H + c * D, D)],
                                                start=(c == 0), stop=(c == 1))
                last.then_inc(v2_in_psum, 1)

            def node_sum(s):
                r, h = s.slot(RING), s.slot(2)
                wait(h2_ready, s.n(1, 1))
                if s.trip is not None or s.at >= 1:
                    wait(added, s.n())
                for j in range(T):
                    last = nc.tensor.matmul(p_sum[:, h * D:(h + 1) * D], onehot[:, s.slot(AHEAD), j, :], h2[:, r, j, :],
                                            start=(j == 0), stop=(j == T - 1))
                last.then_inc(summed, 1)

            pipeline(pe, GROUPS, AHEAD, [(1, turn_ea), (8, node_sum), (2, first_product), (5, second_product),
                                         (4, turn_v)])

        @block.scalar
        def _(act):
            wait = Waits(act, woken["act"])
            A = nc.scalar

            def copy_ea(s):
                r = s.slot(RING)
                wait(ea1_turned, s.n(1, 1))
                A.copy(ea1_t[:, r, :], p_ea[s.slot(2)][0:EA + 1, 0:T * P]).then_inc(ea1t_ready, 1)

            def deviation(s, k, source, ready, width, squared, made):
                r = s.slot(RING)
                wait(ready, s.n(1, 1))
                for j in range(T):
                    A.activation(junk[:, r, k, j, 0:width], source[:, r, j, :], ACT.Square, bias=zero_s[:, 0:1],
                                 accum_out=sq[:, r, k, j:j + 1]).then_inc(squared, 1)
                wait(squared, s.n(T, T))
                A.activation(dev[:, r, k, :], sq[:, r, k, :], ACT.Sqrt, bias=eps_s[:, 0:1],
                             scale=1.0 / width).then_inc(made, 1)

            def deviation1(s):
                deviation(s, 0, v, v_ready, H, sq1_done, dev1_ready)

            def deviation2(s):
                deviation(s, 1, v2, v2_ready, D, sq2_done, dev2_ready)

            def relu1(s):
                r, h = s.slot(RING), s.slot(2)
                d = act.value_load(tab_s[0:1, 1, bass.ds(s.n(), 1)], min_val=0, max_val=1)
                wait(v_turned, s.n(1, 1))
                gb1 = w["gb1"][:, :, :].rearrange("p d c -> p (d c)")
                for c in range(2):
                    last = A.activation(h_t[:, r, c, :], p_turn[h][:, c * T * P:(c + 1) * T * P], ACT.Relu,
                                        bias=gb1[:, bass.ds(d * 4 + 2 + c, 1)], scale=gb1[:, bass.ds(d * 4 + c, 1)])
                last.then_inc(ht_ready, 1)

            pipeline(act, GROUPS, AHEAD, [(5, relu1), (6, deviation2), (1, copy_ea), (3, deviation1)])

        @block.vector
        def _(dve):
            wait = Waits(dve, woken["dve"])
            V = nc.vector
            V.memset(acc[:, :, :], 0.0).then_inc(cleared, 1)
            V.memset(ea1[:, :, :, EA:EA + 1], 1.0).then_inc(cleared, 1)
            dve.wait_ge(cleared, 2)
            rows = w["rows"]

            def row(base, d):
                return rows[:, :, :].rearrange("p i f -> p (i f)")[:, bass.ds(d * D + base * D, D)].unsqueeze(1)\
                    .to_broadcast([P, T, D])

            def take(s):
                r = s.slot(AHEAD)
                wait(rec_in[r], s.turn(AHEAD, 16, 16))
                V.tensor_copy(index[:, r, :], rec[:, r, :, R_COL]).then_inc(index_ready, 1)
                for j in range(T):
                    last = V.tensor_scalar(ea1[:, s.slot(RING), j, 0:EA], rec[:, r, j, 0:EA], rec[:, r, j, R_ATT:R_ATT + 1],
                                           None, ALU.mult)
                last.then_inc(ea1_ready, 1)

            def join(s):
                r, h = s.slot(AHEAD), s.slot(2)
                wait(u_in[r], s.turn(AHEAD, 16 * T, 16 * T))
                wait(v_in_psum, s.n(1, 1))
                for j in range(T):
                    last = V.scalar_tensor_tensor(out=v[:, s.slot(RING), j, :], in0=u[:, r, j, :],
                                                  scalar=rec[:, r, j, R_ATT:R_ATT + 1],
                                                  in1=p_v[h][:, j * H:(j + 1) * H], op0=ALU.mult, op1=ALU.add)
                last.then_inc(v_ready, 1)
                for j in range(T):
                    last = V.tensor_scalar(onehot[:, r, j, :], iota_f[:, :], rec[:, r, j, R_LOC0:R_LOC0 + 1], None,
                                           ALU.is_equal)
                last.then_inc(rec_used, 1)

            def norm1(s):
                r = s.slot(RING)
                wait(dev1_ready, s.n(1, 1))
                V.reciprocal(inv[:, r, 0, :], dev[:, r, 0, :]).then_inc(inv1_done, 1)
                wait(inv1_done, s.n(1, 1))
                for j in range(T):
                    last = V.tensor_scalar(vn[:, r, j, :], v[:, r, j, :], inv[:, r, 0, j:j + 1], None, ALU.mult)
                last.then_inc(vn_ready, 1)

            def bias2(s):
                r, h = s.slot(RING), s.slot(2)
                d = dve.value_load(tab_s[0:1, 1, bass.ds(s.n(), 1)], min_val=0, max_val=1)
                wait(v2_in_psum, s.n(1, 1))
                V.tensor_tensor(v2[:, r, :, :], p_v2[:, h * T * D:(h + 1) * T * D].rearrange("p (t f) -> p t f", t=T),
                                row(B2, d), ALU.add).then_inc(v2_ready, 1)

            def norm2_relu(s):
                r = s.slot(RING)
                d = dve.value_load(tab_s[0:1, 1, bass.ds(s.n(), 1)], min_val=0, max_val=1)
                wait(dev2_ready, s.n(1, 1))
                V.reciprocal(inv[:, r, 1, :], dev[:, r, 1, :]).then_inc(norm2, 1)
                wait(norm2, s.n(3, 1))
                g2 = rows[:, :, :].rearrange("p i f -> p (i f)")[:, bass.ds(d * D + G2 * D, D)]
                for j in range(T):
                    last = V.scalar_tensor_tensor(out=h2[:, r, j, :], in0=v2[:, r, j, :],
                                                  scalar=inv[:, r, 1, j:j + 1], in1=g2, op0=ALU.mult, op1=ALU.mult)
                last.then_inc(norm2, 1)
                wait(norm2, s.n(3, 2))
                V.tensor_tensor(v2[:, r, :, :], h2[:, r, :, :], row(BE2, d), ALU.add).then_inc(norm2, 1)
                wait(norm2, s.n(3, 3))
                V.tensor_scalar(h2[:, r, :, :], v2[:, r, :, :], 0.0, None, ALU.max)\
                    .then_inc(h2_ready, 1)

            def add(s):
                h = s.slot(2)
                b = dve.value_load(tab_s[0:1, 0, bass.ds(s.n(), 1)], min_val=0, max_val=BINS - 1)
                wait(summed, s.n(1, 1))
                if s.trip is not None or s.at >= 1:
                    wait(added, s.n())
                into = acc[:, bass.ds(b, 1), :]
                V.tensor_tensor(into, into, p_sum[:, h * D:(h + 1) * D].unsqueeze(1), ALU.add).then_inc(added, 1)

            pipeline(dve, GROUPS, AHEAD, [(9, add), (6, bias2), (0, take), (7, norm2_relu), (4, norm1), (3, join)])


def phase_first_nodes(kit, w, acc):
    nc, t, out, dram, woken, x_s, ident, iota_f, eps_s, zero_s, tab_s = kit
    with ExitStack() as ctx:
        def sb(name, shape, dt=F32):
            return ctx.enter_context(nc.sbuf_tensor("n_" + name, shape, dt))

        def ps(name):
            return ctx.enter_context(nc.psum_tensor("n_" + name, [P, 512], F32))

        def sem(name):
            return ctx.enter_context(nc.semaphore(name))

        flow = sb("flow", [P, RING, 2, D])
        xb = sb("xb", [P, RING, DX])
        turned = sb("turned", [P, RING, 3, P])
        pre = sb("pre", [P, RING, 2, D])
        act_ = sb("normed", [P, RING, 2, D])
        y = sb("y", [P, RING, DX])
        x1 = sb("x1", [P, RING, DX])
        junk = sb("junk", [P, RING, 2, D])
        sq, dev, inv = sb("sq", [P, RING, 2]), sb("dev", [P, RING, 2]), sb("inv", [P, RING, 2])
        bn, mv = sb("bn", [P, RING, 6]), sb("mv", [P, RING, 2])
        dev3, inv3 = sb("dev3", [P, RING, 1]), sb("inv3", [P, RING, 1])
        p_turn = [ps(f"p_turn{i}") for i in range(2)]
        p_pre = [ps(f"p_pre{i}") for i in range(2)]
        staged, turn_done, turned_ready = sem("n_staged"), sem("n_turn_done"), sem("n_turned_ready")
        product_done, pre_ready, squared, dev_ready = sem("n_product"), sem("n_pre"), sem("n_squared"), sem("n_dev")
        chain, mv_ready, dev3_ready = sem("n_chain"), sem("n_mv"), sem("n_dev3")
        chain3, x1_ready, kept = sem("n_chain3"), sem("n_x1_ready"), sem("n_kept")
        stored = [sem(f"n_stored{i}") for i in range(RING)]
        block = ctx.enter_context(nc.Block())
        C = 7

        @block.gpsimd
        def _(pool):
            wait = Waits(pool, woken["pool"])

            def stage(s):
                r = s.slot(RING)
                if s.trip is not None or s.at >= RING:
                    wait(mv_ready, s.n(1, 1 - RING))
                for i, base in enumerate((NBLK, 0)):
                    nc.gpsimd.tensor_copy(flow[:, r, i, :].unsqueeze(1), acc[:, bass.ds(s.n(1, base), 1), :])
                nc.gpsimd.tensor_copy(xb[:, r, :].unsqueeze(1), x_s[:, bass.ds(s.n(), 1), :]).then_inc(staged, 1)

            def keep(s):
                r = s.slot(RING)
                wait(x1_ready, s.n(1, 1))
                nc.gpsimd.tensor_copy(x_s[:, bass.ds(s.n(), 1), :], x1[:, r, :].unsqueeze(1)).then_inc(kept, 1)

            pipeline(pool, NBLK, RING, [(3, keep), (0, stage)])

        @block.tensor
        def _(pe):
            wait = Waits(pe, woken["pe"])

            def turn(s):
                r, h = s.slot(RING), s.slot(2)
                wait(staged, s.n(1, 1))
                for i, src in enumerate((flow[:, r, 0, :], flow[:, r, 1, :], xb[:, r, 0:D])):
                    last = nc.tensor.transpose(p_turn[h][:, i * P:(i + 1) * P], src, ident[:, :])
                last.then_inc(turn_done, 1)

            def product(s):
                r, h = s.slot(RING), s.slot(2)
                wait(turned_ready, s.n(1, 1))
                if s.trip is not None or s.at >= 2:
                    wait(pre_ready, s.n(1, -1))
                for i in range(2):
                    nc.tensor.matmul(p_pre[h][:, 0:D], turned[:, r, i, :], w["nsw"][:, i, :], start=(i == 0),
                                     stop=(i == 1))
                nc.tensor.matmul(p_pre[h][:, D:2 * D], turned[:, r, 2, :], w["nsw"][:, 2, :], start=True, stop=True)\
                    .then_inc(product_done, 1)

            pipeline(pe, NBLK, RING, [(1, product), (0, turn)])

        @block.scalar
        def _(act):
            wait = Waits(act, woken["act"])
            A = nc.scalar

            def copy(s):
                r, h = s.slot(RING), s.slot(2)
                wait(turn_done, s.n(1, 1))
                A.copy(turned[:, r, :, :].rearrange("p i f -> p (i f)"), p_turn[h][:, 0:3 * P])\
                    .then_inc(turned_ready, 1)

            def deviation(s):
                r = s.slot(RING)
                wait(pre_ready, s.n(1, 1))
                for i in range(2):
                    A.activation(junk[:, r, i, :], pre[:, r, i, :], ACT.Square, bias=zero_s[:, 0:1],
                                 accum_out=sq[:, r, i:i + 1]).then_inc(squared, 1)
                wait(squared, s.n(2, 2))
                A.activation(dev[:, r, :], sq[:, r, :], ACT.Sqrt, bias=eps_s[:, 0:1], scale=1.0 / D)\
                    .then_inc(dev_ready, 1)

            def deviation3(s):
                r = s.slot(RING)
                wait(mv_ready, s.n(1, 1))
                A.activation(dev3[:, r, :], mv[:, r, 1:2], ACT.Sqrt, bias=eps_s[:, 0:1]).then_inc(dev3_ready, 1)

            pipeline(act, NBLK, RING, [(2, deviation3), (1, deviation), (0, copy)])

        @block.vector
        def _(dve):
            wait = Waits(dve, woken["dve"])
            V = nc.vector
            rows = w["rows"]

            def biased(s):
                r, h = s.slot(RING), s.slot(2)
                wait(product_done, s.n(1, 1))
                V.tensor_tensor(pre[:, r, :, :], p_pre[h][:, 0:2 * D].rearrange("p (i f) -> p i f", i=2),
                                rows[:, NSB:NSB + 2, :], ALU.add).then_inc(pre_ready, 1)

            def mix(s):
                r = s.slot(RING)
                links = [0]

                def link(ins):
                    links[0] += 1
                    ins.then_inc(chain, 1)
                    wait(chain, s.n(C, links[0]))

                wait(dev_ready, s.n(1, 1))
                link(V.reciprocal(inv[:, r, :], dev[:, r, :]))
                for i in range(2):
                    last = V.scalar_tensor_tensor(out=act_[:, r, i, :], in0=pre[:, r, i, :], scalar=inv[:, r, i:i + 1],
                                                  in1=rows[:, NSG + i, :], op0=ALU.mult, op1=ALU.mult)
                link(last)
                link(V.tensor_tensor(pre[:, r, :, :], act_[:, r, :, :], rows[:, NSBE:NSBE + 2, :], ALU.add))
                link(V.tensor_scalar(act_[:, r, :, :], pre[:, r, :, :], 0.0, None, ALU.max))
                link(V.tensor_tensor(act_[:, r, 0, :], act_[:, r, 0, :], act_[:, r, 1, :], ALU.add))
                V.tensor_tensor(y[:, r, 0:D], act_[:, r, 0, :], xb[:, r, 0:D], ALU.add)
                link(V.tensor_scalar(y[:, r, D:DX], xb[:, r, D:DX], 2.0, None, ALU.mult))
                link(V.bn_stats(bn[:, r, :], y[:, r, :]))
                V.bn_aggr(mv[:, r, :], bn[:, r, :]).then_inc(mv_ready, 1)

            def norm3(s):
                r = s.slot(RING)
                wait(dev3_ready, s.n(1, 1))
                wait(stored[r], s.turn(RING, 32))
                if s.trip is not None or s.at >= RING:
                    wait(kept, s.n(1, 1 - RING))
                V.reciprocal(inv3[:, r, :], dev3[:, r, :]).then_inc(chain3, 1)
                wait(chain3, s.n(1, 1))
                V.tensor_scalar(x1[:, r, :], y[:, r, :], mv[:, r, 0:1], inv3[:, r, :], ALU.subtract, ALU.mult)\
                    .then_inc(x1_ready, 1)

            pipeline(dve, NBLK, RING, [(3, norm3), (2, mix), (1, biased)])

        @block.sync
        def _(sp):
            wait = Waits(sp, woken["sp"])

            def store(s):
                r = s.slot(RING)
                wait(x1_ready, s.n(1, 1))
                for d in range(2):
                    sp.dma_start(dram["x1"][bass.ds(s.n(P, d * NPAD), P), :], x1[:, r, :]).then_inc(stored[r], 16)

            pipeline(sp, NBLK, RING, [(0, store)])
            for r in range(RING):
                wait(stored[r], 32 * len(range(r, NBLK, RING)))


def phase_second_edges(kit, acc, rec_in, x_in):
    nc, t, out, dram, woken, x_s, ident, iota_f, eps_s, zero_s, tab_s = kit
    T = TPG
    BANK = 512
    with ExitStack() as ctx:
        def sb(name, shape, dt=F32):
            return ctx.enter_context(nc.sbuf_tensor("m_" + name, shape, dt))

        def ps(name):
            return ctx.enter_context(nc.psum_tensor("m_" + name, [P, BANK], F32))

        def sem(name):
            return ctx.enter_context(nc.semaphore(name))

        rec = sb("rec", [P, AHEAD, T, RW])
        index = sb("index", [P, AHEAD, T], I32)
        q = sb("q", [P, AHEAD, T, QW])
        prod = sb("prod", [P, RING, T, 3 * M1])
        onehot = sb("onehot", [P, RING, T, P])
        p_lo = [ps(f"p_lo{i}") for i in range(2)]
        p_hi = [ps(f"p_hi{i}") for i in range(2)]
        loads = GROUPS // AHEAD * 16
        gathers = GROUPS // AHEAD * 16 * T
        rec_used, index_ready, cleared = sem("m_rec_used"), sem("m_index_ready"), sem("m_cleared")
        prod_done, q_ready, summed, added = sem("m_prod_done"), sem("m_q_ready"), sem("m_summed"), sem("m_added")
        scaled = sem("m_scaled")
        block = ctx.enter_context(nc.Block())

        @block.sync
        def _(sp):
            wait = Waits(sp, woken["sp"])

            def load(s):
                r = s.slot(AHEAD)
                wait(rec_used, s.n(1, 1 - AHEAD))
                if s.trip is not None or s.at >= AHEAD:
                    wait(scaled, s.n(1, 1 - AHEAD))
                sp.dma_start(rec[:, r, :, :].rearrange("p t w -> p (t w)"),
                             dram["rec"].rearrange("(g p t) w -> g p (t w)", p=P, t=T)[bass.ds(s.n(), 1), :, :]
                             .rearrange("g p w -> (g p) w")).then_inc(rec_in[r], 16)

            pipeline(sp, GROUPS, AHEAD, [(0, load)])

        @block.gpsimd
        def _(pool):
            wait = Waits(pool, woken["pool"])

            def gather(s):
                r = s.slot(AHEAD)
                wait(index_ready, s.n(1, 1))
                for j in range(T):
                    nc.gpsimd.indirect_dma_start(
                        q[:, r, j, 0:DX], None, dram["x1"],
                        bass.IndirectOffsetOnAxis(ap=index[:, r, j:j + 1], axis=0)).then_inc(x_in[r], 16)

            pipeline(pool, GROUPS, AHEAD, [(0, gather)])

        @block.scalar
        def _(act):
            wait = Waits(act, woken["act"])

            def scale(s):
                r = s.slot(AHEAD)
                wait(x_in[r], s.turn(AHEAD, 16 * T, 16 * T + gathers))
                for j in range(T):
                    last = nc.scalar.mul(q[:, r, j, Q_E0:Q_E0 + DX], q[:, r, j, 0:DX], rec[:, r, j, R_E0:R_E0 + 1])
                last.then_inc(scaled, 1)

            pipeline(act, GROUPS, AHEAD, [(3, scale)])

        @block.tensor
        def _(pe):
            wait = Waits(pe, woken["pe"])

            def node_sum(s):
                r, h = s.slot(AHEAD), s.slot(2)
                wait(q_ready, s.n(1, 1))
                wait(scaled, s.n(1, 1))
                if s.trip is not None or s.at >= 2:
                    wait(added, s.n(1, -1))
                for p, lo, hi in ((p_lo[h], 0, BANK), (p_hi[h], BANK, QW)):
                    for j in range(T):
                        last = nc.tensor.matmul(p[:, 0:hi - lo], onehot[:, s.slot(RING), j, :], q[:, r, j, lo:hi],
                                                start=(j == 0), stop=(j == T - 1))
                last.then_inc(summed, 1)

            pipeline(pe, GROUPS, AHEAD, [(4, node_sum)])

        @block.vector
        def _(dve):
            wait = Waits(dve, woken["dve"])
            V = nc.vector
            V.memset(acc[:, :, :], 0.0).then_inc(cleared, 1)
            dve.wait_ge(cleared, 1)

            def take(s):
                r = s.slot(AHEAD)
                wait(rec_in[r], s.turn(AHEAD, 16, 16 + loads))
                V.tensor_copy(index[:, r, :], rec[:, r, :, R_COL]).then_inc(index_ready, 1)

            def spread(s):
                r = s.slot(AHEAD)
                wait(x_in[r], s.turn(AHEAD, 16 * T, 16 * T + gathers))
                e1 = rec[:, r, :, R_E1:R_E1 + 3]
                V.tensor_tensor(prod[:, s.slot(RING), :, :].rearrange("p t (u k) -> p t u k", k=3),
                                q[:, r, :, M0:DX].rearrange("p t (u k) -> p t u k", k=3),
                                e1.unsqueeze(2).to_broadcast([P, T, M1, 3]), ALU.mult).then_inc(prod_done, 1)
                for j in range(T):
                    V.tensor_scalar(onehot[:, s.slot(RING), j, :], iota_f[:, :], rec[:, r, j, R_LOC1:R_LOC1 + 1], None,
                                    ALU.is_equal)
                last = V.tensor_tensor(q[:, r, :, Q_E1:Q_Z].rearrange("p t (k u) -> p t k u", k=3),
                                       q[:, r, :, 0:M0].unsqueeze(2).to_broadcast([P, T, 3, M0]),
                                       e1.unsqueeze(3).to_broadcast([P, T, 3, M0]), ALU.mult)
                last.then_inc(rec_used, 1)
                wait(prod_done, s.n(1, 1))
                V.reduce_sum(q[:, r, :, Q_Z:QW], prod[:, s.slot(RING), :, :].rearrange("p t (u k) -> p t u k", k=3),
                             axis=AX_X).then_inc(q_ready, 1)

            def add(s):
                h = s.slot(2)
                b = dve.value_load(tab_s[0:1, 2, bass.ds(s.n(), 1)], min_val=0, max_val=NBLK - 1)
                wait(summed, s.n(1, 1))
                if s.trip is not None or s.at >= 1:
                    wait(added, s.n())
                for p, lo, hi in ((p_lo[h], 0, BANK), (p_hi[h], BANK, QW)):
                    into = acc[:, bass.ds(b, 1), lo:hi]
                    last = V.tensor_tensor(into, into, p[:, 0:hi - lo].unsqueeze(1), ALU.add)
                last.then_inc(added, 1)

            pipeline(dve, GROUPS, AHEAD, [(5, add), (0, take), (3, spread)])


def phase_second_nodes(kit, acc):
    nc, t, out, dram, woken, x_s, ident, iota_f, eps_s, zero_s, tab_s = kit
    F0, F1 = M0 * M0 + M1 * M1, 2 * M0 * M1
    c_msg = (M0 + M1) ** -0.5
    c0, c1 = F0 ** -0.5, F1 ** -0.5
    inv3_ = 3.0 ** -0.5
    QC = -(-QW // P)
    with ExitStack() as ctx:
        def sb(name, shape, dt=F32):
            return ctx.enter_context(nc.sbuf_tensor("f_" + name, shape, dt))

        def ps(name):
            return ctx.enter_context(nc.psum_tensor("f_" + name, [P, 512], F32))

        def sem(name):
            return ctx.enter_context(nc.semaphore(name))

        mix_w = sb("mix_w", [P, QC, DX])
        lin_w = sb("lin_w", [P, 2, DX])
        w000 = sb("w000", [M0, M0 * M0])
        w011 = sb("w011", [M0, M1 * M1])
        w101 = sb("w101", [M0, M1 * M1])
        w110 = sb("w110", [P, M1 * M1 // P, M0])
        xb = sb("xb", [P, 2, DX])
        gb = sb("gb", [P, 1, QW])
        x_t = sb("x_t", [P, 1, 2, P])
        g_t = sb("g_t", [P, 1, QC, P])
        agg = sb("agg", [P, 2, DX])
        a_t = sb("a_t", [M0, 1, P])
        outer = sb("outer", [P, M1 * M1])
        outer2 = sb("outer2", [P, M1 * M1])
        o_t = sb("o_t", [P, M1 * M1 // P, P])
        m0 = sb("m0", [P, M0 // 2, M0])
        m1 = m0[:, :, :].rearrange("p v w -> p (v w)").rearrange("p (v w) -> p v w", w=M1)
        red0 = sb("red0", [P, 2, M0])
        red = sb("red", [P, 2, DX])
        y = sb("y", [P, 2, DX])
        fin = sb("fin", [P, 2, DX])
        bn, mv, dev, inv = sb("bn", [P, 2, 6]), sb("mv", [P, 2, 2]), sb("dev", [P, 2, 1]), sb("inv", [P, 2, 1])
        raw = sb("raw", [M0, 7, M0])
        p_x = ps("p_x")
        p_g = ps("p_g")
        p_m = ps("p_m")
        p_b = [ps(f"p_b{i}") for i in range(5)]

        loaded, zeroed, laid, mixed = sem("w_loaded"), sem("w_zeroed"), sem("w_laid"), sem("w_mixed")
        chain0 = sem("w_chain")
        staged, g_turned, xt_ready = sem("f_staged"), sem("f_g_turned"), sem("f_xt_ready")
        gt_ready, agg_done, agg_ready = sem("f_gt_ready"), sem("f_agg_done"), sem("f_agg_ready")
        a_turned, at_ready = sem("f_a_turned"), sem("f_at_ready")
        bank_full, bank_free = sem("f_bank_full"), sem("f_bank_free")
        outer_step, outer_ready = sem("f_outer_step"), sem("f_outer_ready")
        o_turned, ot_ready, linear_done = sem("f_o_turned"), sem("f_ot_ready"), sem("f_linear_done")
        chain, mv_ready, dev_ready = sem("f_chain"), sem("f_mv_ready"), sem("f_dev_ready")
        inv_done, fin_ready = sem("f_inv_done"), sem("f_fin_ready")
        stored = [sem(f"f_stored{i}") for i in range(2)]
        o_half = sem("f_o_half")

        L = "L1_gnn_"
        small = [("lm0", M0, M0, M0 ** -0.5), ("lm1", M1, M1, M1 ** -0.5), ("wm000", M0, M0, c_msg),
                 ("wm101", M1, M1, c_msg), ("wm011", M0, M1, c_msg), ("wm110", M1, M0, c_msg * inv3_),
                 ("lu0", M0, M0, M0 ** -0.5), ]
        small2 = [("lu1", M1, M1, M1 ** -0.5)]
        raw2 = sb("raw2", [M1, M1])

        with nc.Block() as block:
            mix = dram["mix"]

            def vec(base, k, rows, first_col):
                return mix[base:base + 3 * rows, :].rearrange("(u k) c -> k u c", k=3)[k, :, first_col:DX]\
                    .rearrange("u (w k) -> k u w", k=3)[k]

            @block.vector
            def _(dve):
                n = [0]

                def link(ins):
                    n[0] += 1
                    ins.then_inc(chain0, 1)
                    dve.wait_ge(chain0, n[0])

                nc.vector.memset(g_t[:, :, :, :], 0.0).then_inc(zeroed, 1)
                nc.vector.memset(mix_w[:, :, :], 0.0).then_inc(zeroed, 1)
                nc.vector.memset(lin_w[:, :, :], 0.0).then_inc(zeroed, 1)
                dve.wait_ge(loaded, 16 * 13)
                for i, (name, k, m, scale) in enumerate(small):
                    nc.vector.tensor_scalar(raw[0:k, i, 0:m], raw[0:k, i, 0:m], scale, None, ALU.mult)\
                        .then_inc(mixed, 1)
                nc.vector.tensor_scalar(raw2[:, :], raw2[:, :], M1 ** -0.5, None, ALU.mult).then_inc(mixed, 1)
                nc.vector.tensor_scalar(w000[:, :], w000[:, :], c0, None, ALU.mult)
                nc.vector.tensor_scalar(w011[:, :], w011[:, :], c1, None, ALU.mult)
                nc.vector.tensor_scalar(w101[:, :], w101[:, :], c1, None, ALU.mult)
                nc.vector.tensor_scalar(w110[:, :, :], w110[:, :, :], c0 * inv3_, None, ALU.mult)

            @block.sync
            def _(sp):
                for i, (name, k, m, scale) in enumerate(small):
                    src = t[L + name]
                    if len(src.shape) == 3:
                        src = src.rearrange("u o w -> u (o w)")
                    sp.dma_start(raw[0:k, i, 0:m], src).then_inc(loaded, 16)
                sp.dma_start(raw2[:, :], t[L + "lu1"]).then_inc(loaded, 16)
                sp.dma_start(w000[:, :], t[L + "wu000"].rearrange("u v w -> u (v w)")).then_inc(loaded, 16)
                sp.dma_start(w011[:, :], t[L + "wu011"].rearrange("u v w -> u (v w)")).then_inc(loaded, 16)
                sp.dma_start(w101[:, :].rearrange("v (u w) -> v u w", u=M1),
                             t[L + "wu101"].rearrange("u v w -> v u w")).then_inc(loaded, 16)
                sp.dma_start(w110[:, :, :], t[L + "wu110"].rearrange("u v w -> (u v) w")
                             .rearrange("(c k) w -> k c w", k=P)).then_inc(loaded, 16)
                sp.dma_start(red[:, 0, :], t["x"][0:P, :]).then_inc(loaded, 16)
                sp.wait_ge(zeroed, 2)
                zeros = mix_w[:, :, :].rearrange("p c f -> p (c f)")
                rows = 88
                for half in range(2):
                    sp.dma_start(mix.rearrange("(h p r) c -> h p (r c)", h=2, p=rows)[half],
                                 zeros[0:rows, 0:(QW + DX) // (2 * rows) * DX]).then_inc(laid, 16)
                sp.wait_ge(laid, 32)
                sp.wait_ge(mixed, 8)
                placed = [(mix[0:M0, 0:M0], raw[:, 0, :]), (mix[Q_E0:Q_E0 + M0, 0:M0], raw[:, 2, :]),
                          (mix[Q_Z:QW, 0:M0], raw[0:M1, 5, :]), (mix[QW:QW + M0, 0:M0], raw[:, 6, :])]
                for k in range(3):
                    placed += [(vec(M0, k, M1, M0), raw[0:M1, 1, 0:M1]),
                               (vec(Q_E0 + M0, k, M1, M0), raw[0:M1, 3, 0:M1]),
                               (mix[Q_E1 + k * M0:Q_E1 + (k + 1) * M0, M0:DX].rearrange("u (w k) -> k u w", k=3)[k],
                                raw[:, 4, 0:M1]),
                               (vec(QW + M0, k, M1, M0), raw2[:, :])]
                for dst, src in placed:
                    sp.dma_start(dst, src).then_inc(laid, 16)
                sp.wait_ge(laid, 16 * (2 + len(placed)))
                n = 2 + len(placed)
                for dst, base, rows in ((mix_w, 0, QW), (lin_w, QW, DX)):
                    for c in range(-(-rows // P)):
                        k = min(P, rows - c * P)
                        sp.dma_start(dst[0:k, c, :], mix[base + c * P:base + c * P + k, :]).then_inc(laid, 16)
                        n += 1
                sp.wait_ge(laid, 16 * n)

        BANKS = 12
        NPB = len(p_b)
        CH = 10
        with nc.Block() as block:
            @block.gpsimd
            def _(pool):
                wait = Waits(pool, woken["pool"])
                G = nc.gpsimd

                def stage(s):
                    h = s.slot(2)
                    if s.trip is not None or s.at >= 2:
                        wait(mv_ready, s.n(1, -1))
                        wait(gt_ready, s.n())
                    G.tensor_copy(xb[:, h, :].unsqueeze(1), x_s[:, bass.ds(s.n(), 1), :])
                    G.tensor_copy(gb[:, 0, :].unsqueeze(1), acc[:, bass.ds(s.n(), 1), :]).then_inc(staged, 1)

                def outer_product(s):
                    h = s.slot(2)
                    wait(agg_ready, s.n(1, 1))
                    if s.trip is not None or s.at >= 1:
                        wait(o_turned, s.n())
                    x1 = xb[:, h, M0:DX].rearrange("p (u k) -> p u k", k=3)
                    a1 = agg[:, h, M0:DX].rearrange("p (v k) -> p v k", k=3)

                    def term(dst, k):
                        return G.tensor_tensor(dst.rearrange("p (u v) -> p u v", u=M1),
                                               x1[:, :, k:k + 1].to_broadcast([P, M1, M1]),
                                               a1[:, :, k].unsqueeze(1).to_broadcast([P, M1, M1]), ALU.mult)

                    term(outer[:, :], 0)
                    term(outer2[:, :], 1).then_inc(outer_step, 1)
                    wait(outer_step, s.n(3, 1))
                    G.tensor_tensor(outer[:, :], outer[:, :], outer2[:, :], ALU.add).then_inc(outer_step, 1)
                    wait(outer_step, s.n(3, 2))
                    term(outer2[:, :], 2).then_inc(outer_step, 1)
                    wait(outer_step, s.n(3, 3))
                    G.tensor_tensor(outer[:, :], outer[:, :], outer2[:, :], ALU.add).then_inc(outer_ready, 1)

                pipeline(pool, NBLK, 2, [(1, outer_product), (0, stage)])

            @block.tensor
            def _(pe):
                wait = Waits(pe, woken["pe"])
                M = nc.tensor.matmul

                def turn(s):
                    h = s.slot(2)
                    wait(staged, s.n(1, 1))
                    nc.tensor.transpose(p_x[:, 0:P], xb[:, h, 0:P], ident[:, :])
                    nc.tensor.transpose(p_x[0:DX - P, P:2 * P], xb[:, h, P:DX], ident[:, :])
                    for c in range(QC):
                        k = min(P, QW - c * P)
                        p, at = (p_g, c * P) if c < 4 else (p_x, 2 * P)
                        last = nc.tensor.transpose(p[0:k, at:at + P], gb[:, 0, c * P:c * P + k], ident[:, :])
                    last.then_inc(g_turned, 1)

                def aggregate(s):
                    h = s.slot(2)
                    wait(gt_ready, s.n(1, 1))
                    for c in range(QC):
                        last = M(p_g[:, 0:DX], g_t[:, 0, c, :], mix_w[:, c, :], start=(c == 0), stop=(c == QC - 1))
                    last.then_inc(agg_done, 1)

                def turn_a(s):
                    h = s.slot(2)
                    wait(agg_ready, s.n(1, 1))
                    nc.tensor.transpose(p_x[0:M0, 3 * P:4 * P], agg[:, h, 0:M0], ident[:, :]).then_inc(a_turned, 1)

                def bank(s, i, lhs, rhs, n):
                    b = p_b[i % NPB]
                    M(b[:, 0:n], lhs, rhs, start=True, stop=True).then_inc(bank_full, 1)

                def banks(s):
                    h = s.slot(2)
                    wait(xt_ready, s.n(1, 1))
                    for i in range(BANKS):
                        if i >= NPB or s.trip is not None or s.at >= 1:
                            held = i - NPB if i >= NPB else max(range(i, BANKS, NPB)) - BANKS
                            wait(bank_free, s.n(BANKS, held + 1))
                        if i < 8:
                            bank(s, i, x_t[0:M0, 0, 0, :], w000[:, i * 512:(i + 1) * 512], 512)
                        elif i < 10:
                            bank(s, i, x_t[0:M0, 0, 0, :], w011[:, (i - 8) * 512:(i - 7) * 512], 512)
                        else:
                            if i == 10:
                                wait(at_ready, s.n(1, 1))
                            bank(s, i, a_t[:, 0, :], w101[:, (i - 10) * 512:(i - 9) * 512], 512)

                def turn_outer(s):
                    wait(outer_ready, s.n(1, 1))
                    for i in range(8):
                        b = p_g if i < 4 else p_x
                        last = nc.tensor.transpose(b[:, (i % 4) * P:(i % 4 + 1) * P], outer[:, i * P:(i + 1) * P],
                                                   ident[:, :])
                        if i % 4 == 3:
                            last.then_inc(o_turned if i == 7 else o_half, 1)

                def linear(s):
                    h = s.slot(2)
                    wait(ot_ready, s.n(2, 2))
                    if s.trip is not None or s.at >= 1:
                        wait(chain, s.n(CH, 8 - CH))
                    M(p_m[:, 0:DX], x_t[:, 0, 0, :], lin_w[:, 0, :], start=True, stop=False, skip_group_check=True)
                    M(p_m[:, 0:DX], x_t[0:DX - P, 0, 1, :], lin_w[0:DX - P, 1, :], start=False, stop=False,
                      skip_group_check=True)
                    for i in range(8):
                        last = M(p_m[:, 0:M0], o_t[:, i, :], w110[:, i, :], start=False, stop=(i == 7),
                                 skip_group_check=True)
                    last.then_inc(linear_done, 1)

                def all_of(s):
                    if s.trip is not None or s.at >= 1:
                        wait(ot_ready, s.n(2))
                    turn(s)
                    aggregate(s)
                    turn_a(s)
                    banks(s)
                    turn_outer(s)
                    linear(s)

                pipeline(pe, NBLK, 2, [(0, all_of)])

            @block.scalar
            def _(act):
                wait = Waits(act, woken["act"])
                A = nc.scalar

                def copies(s):
                    h = s.slot(2)
                    wait(g_turned, s.n(1, 1))
                    A.copy(x_t[:, 0, 0, :], p_x[:, 0:P])
                    A.copy(x_t[0:DX - P, 0, 1, :], p_x[0:DX - P, P:2 * P]).then_inc(xt_ready, 1)
                    A.copy(g_t[:, 0, 0:4, :].rearrange("p c n -> p (c n)"), p_g[:, :])
                    A.copy(g_t[0:QW - 4 * P, 0, 4, :], p_x[0:QW - 4 * P, 2 * P:3 * P]).then_inc(gt_ready, 1)
                    wait(agg_done, s.n(1, 1))
                    A.copy(agg[:, h, :], p_g[:, 0:DX]).then_inc(agg_ready, 1)
                    wait(a_turned, s.n(1, 1))
                    A.copy(a_t[:, 0, :], p_x[0:M0, 3 * P:4 * P]).then_inc(at_ready, 1)

                def copies2(s):
                    wait(o_half, s.n(1, 1))
                    A.copy(o_t[:, 0:4, :].rearrange("p c n -> p (c n)"), p_g[:, :]).then_inc(ot_ready, 1)
                    wait(o_turned, s.n(1, 1))
                    A.copy(o_t[:, 4:8, :].rearrange("p c n -> p (c n)"), p_x[:, :]).then_inc(ot_ready, 1)

                def deviation(s):
                    h = s.slot(2)
                    wait(mv_ready, s.n(1, 1))
                    A.activation(dev[:, h, :], mv[:, h, 1:2], ACT.Sqrt, bias=eps_s[:, 0:1]).then_inc(dev_ready, 1)

                pipeline(act, NBLK, 2, [(0, copies), (1, deviation), (0, copies2)])

            @block.vector
            def _(dve):
                wait = Waits(dve, woken["dve"])
                V = nc.vector

                def main(s):
                    h = s.slot(2)
                    links = [0]

                    def link(ins):
                        links[0] += 1
                        ins.then_inc(chain, 1)
                        wait(chain, s.n(CH, links[0]))

                    wait(agg_ready, s.n(1, 1))
                    for half in range(2):
                        for i in range(4 * half, 4 * half + 4):
                            wait(bank_full, s.n(BANKS, i + 1))
                            V.tensor_tensor(m0[:, (i % 4) * 8:(i % 4 + 1) * 8, :],
                                            p_b[i % NPB][:, :].rearrange("p (v w) -> p v w", w=M0),
                                            agg[:, h, i * 8:(i + 1) * 8].unsqueeze(2).to_broadcast([P, 8, M0]),
                                            ALU.mult).then_inc(bank_free, 1)
                        wait(bank_free, s.n(BANKS, 4 * half + 4))
                        link(V.reduce_sum(red0[:, half, :], m0[:, :, :].rearrange("p v w -> p w v"), axis=AX_X))
                    V.tensor_tensor(red[:, h, 0:M0], red0[:, 0, :], red0[:, 1, :], ALU.add)
                    a1 = agg[:, h, M0:DX].rearrange("p (v k) -> p v k", k=3)
                    x1 = xb[:, h, M0:DX].rearrange("p (u k) -> p u k", k=3)
                    wait(bank_full, s.n(BANKS, 12))
                    for k in range(3):
                        for i in range(4):
                            c = (a1 if i < 2 else x1)[:, (i % 2) * 16:(i % 2 + 1) * 16, k:k + 1]
                            last = V.tensor_tensor(m1[:, i * 16:(i + 1) * 16, :],
                                                   p_b[(8 + i) % NPB][:, :].rearrange("p (v w) -> p v w", w=M1),
                                                   c.to_broadcast([P, 16, M1]), ALU.mult)
                            if k == 2:
                                last.then_inc(bank_free, 1)
                        link(last) if k < 2 else wait(bank_free, s.n(BANKS, 12))
                        ins = V.reduce_sum(red[:, h, M0:DX].rearrange("p (w k) -> p k w", k=3)[:, k, :],
                                           m1.rearrange("p v w -> p w v"), axis=AX_X)
                        link(ins)
                    wait(linear_done, s.n(1, 1))
                    link(V.tensor_tensor(red[:, h, :], red[:, h, :], p_m[:, 0:DX], ALU.add))
                    link(V.scalar_tensor_tensor(out=y[:, h, :], in0=xb[:, h, :], scalar=2.0, in1=red[:, h, :],
                                                op0=ALU.mult, op1=ALU.add))
                    link(V.bn_stats(bn[:, h, :], y[:, h, :]))
                    V.bn_aggr(mv[:, h, :], bn[:, h, :]).then_inc(mv_ready, 1)
                    assert links[0] == CH

                def final(s):
                    h = s.slot(2)
                    wait(dev_ready, s.n(1, 1))
                    wait(stored[h], s.turn(2, 16))
                    V.reciprocal(inv[:, h, :], dev[:, h, :]).then_inc(inv_done, 1)
                    wait(inv_done, s.n(1, 1))
                    V.tensor_scalar(fin[:, h, :], y[:, h, :], mv[:, h, 0:1], inv[:, h, :], ALU.subtract,
                                    ALU.mult).then_inc(fin_ready, 1)

                pipeline(dve, NBLK, 2, [(0, main), (1, final)])

            @block.sync
            def _(sp):
                wait = Waits(sp, woken["sp"])

                def store(s):
                    h = s.slot(2)
                    wait(fin_ready, s.n(1, 1))
                    sp.dma_start(out[bass.ds(s.n(P), P), :], fin[:, h, :]).then_inc(stored[h], 16)

                pipeline(sp, NBLK - 1, 2, [(0, store)])
                last = NBLK - 1
                wait(fin_ready, NBLK)
                sp.dma_start(out[last * P:N, :], fin[0:NLAST, last % 2, :]).then_inc(stored[last % 2], 16)
                for h in range(2):
                    wait(stored[h], 16 * len(range(h, NBLK, 2)))


def kernel(**inputs):
    import numpy as _np
    import concourse.bacc as _bacc
    from concourse import mybir as _mybir
    from concourse.bass_utils import run_bass_kernel_spmd as _run

    nc = _bacc.Bacc("TRN2", target_bir_lowering=False, num_devices=1)
    arrays, args = {}, {}
    for name in sorted(inputs):
        if name == "node_vec1":
            continue
        a = _np.ascontiguousarray(inputs[name])
        arrays[f"in_{name}_dram"] = a
        args[name] = nc.dram_tensor(f"in_{name}_dram", a.shape, _mybir.dt.from_np(a.dtype), kind="ExternalInput").ap()
    out = nc.dram_tensor("out_0_dram", (N, DX), _mybir.dt.float32, kind="ExternalOutput").ap()
    build(nc, args, out)
    r = _run(nc, [arrays], core_ids=[0])
    return r.results[0]["out_0_dram"]
```

```python
from contextlib import ExitStack

import concourse.bass as bass
from concourse import mybir

F32 = mybir.dt.float32
I32 = mybir.dt.int32
BF16 = mybir.dt.bfloat16
ALU = mybir.AluOpType
ACT = mybir.ActivationFunctionType
AX_X = mybir.AxisListType.X
RMAX = bass.bass_isa.ReduceOp.max
RADD = bass.bass_isa.ReduceOp.add

P = 128
N = 6250
NBLK = -(-N // P)
NPAD = NBLK * P
NLAST = N - (NBLK - 1) * P
E = 106250
EP = 125
ET = E // EP
D = 128
DX = 160
EA = 64
H = 256
BINS = 2 * NBLK
TPG = 2
SLOTS = TPG * P
GROUPS = (E + BINS * (SLOTS - 1)) // SLOTS
M0, M1 = 64, 32
CHUNK = 512
LINE = 4
CHUNKS = 208
PER_CHUNK = ET // CHUNKS
assert PER_CHUNK == 4
LN_EPS = 1e-5
SLOPE = 0.01
BIG = 1e30

R_EA, R_E1, R_E0, R_ATT, R_LOC1, R_LOC0, R_COL = 0, 64, 67, 68, 69, 70, 71
RW = 72
Q_X, Q_E0, Q_E1, Q_Z = 0, DX, 2 * DX, 2 * DX + 3 * M0
QW = Q_Z + M1

RING = 4
PAIR = 2
AHEAD = 8


class Step:

    def __init__(self, trip, at):
        self.trip, self.at = trip, at

    def back(self, lag):
        return Step(self.trip, self.at - lag)

    def n(self, per=1, plus=0):
        if self.trip is None:
            return self.at * per + plus
        return (self.trip * per if per != 1 else self.trip) + (self.at * per + plus)

    def turn(self, ring, per=1, plus=0):
        if self.trip is None:
            return self.at // ring * per + plus
        assert per % ring == 0
        return (self.trip * (per // ring) if per != ring else self.trip) + (self.at // ring * per + plus)

    def slot(self, ring):
        return self.at % ring


def pipeline(eng, total, unroll, stages):
    most = max(lag for lag, _ in stages)
    lead = -(-(most + unroll) // unroll) * unroll
    trips = (total - lead) // unroll

    def body(step):
        for lag, stage in stages:
            if step.trip is not None or 0 <= step.at - lag < total:
                stage(step.back(lag))

    for at in range(lead):
        body(Step(None, at))
    with eng.Fori(lead, lead + (trips - 1) * unroll + 1, unroll) as trip:
        for u in range(unroll):
            body(Step(trip, u))
    for at in range(lead + trips * unroll, total + most):
        body(Step(None, at))


class Waits:

    def __init__(self, eng, woken):
        self.eng, self.woken = eng, woken

    def wait_ge(self, sem, count):
        if isinstance(count, int):
            if count > 0:
                self.eng.wait_ge(sem, count)
        else:
            self.eng.wait_ge(sem, count)
            self.eng.sem_inc(self.woken, 1)


def split(rows):
    cut = rows // 16 * 16
    return [(0, cut), (cut, rows)]


def build(nc, t, out):
    with ExitStack() as ctx:
        ctx.enter_context(nc.allow_non_contiguous_dma(reason="small weights and tables"))

        def sb(name, shape, dt=F32, into=ctx):
            return into.enter_context(nc.sbuf_tensor(name, shape, dt))

        def sem(name):
            return ctx.enter_context(nc.semaphore(name))

        woken = {e: sem(f"woken_{e}") for e in ("sp", "act", "dve", "pe", "pool")}
        dram = {
            "u": nc.dram_tensor("u_table", (2 * NPAD, H), F32).ap(),
            "x1": nc.dram_tensor("x1_table", (2 * NPAD, DX), F32).ap(),
            "a": nc.dram_tensor("a_table", (NPAD, 1), F32).ap(),
            "b": nc.dram_tensor("b_table", (NPAD, 1), F32).ap(),
            "rows": nc.dram_tensor("rows_hi_lo", (2, CHUNKS * CHUNK), BF16).ap(),
            "from_row": nc.dram_tensor("from_row", (CHUNKS * CHUNK, 1), F32).ap(),
            "rec": nc.dram_tensor("records", (GROUPS * SLOTS, RW), F32).ap(),
            "tab": nc.dram_tensor("group_table", (3, GROUPS), I32).ap(),
            "mix": nc.dram_tensor("mix_weights", (QW + DX, DX), F32).ap(),
        }
        x_s = sb("x_s", [P, NBLK, DX])
        ident = sb("ident", [P, P])
        iota_f = sb("iota_f", [P, P])
        eps_s = sb("eps_s", [P, 1])
        zero_s = sb("zero_s", [P, 1])
        tab_s = sb("tab_s", [1, 3, GROUPS], I32)
        kit = (nc, t, out, dram, woken, x_s, ident, iota_f, eps_s, zero_s, tab_s)
        rec_in = [sem(f"rec_in{i}") for i in range(AHEAD)]
        rows_in = [sem(f"rows_in{i}") for i in range(AHEAD)]
        records_clear = sem("records_clear")
        with ExitStack() as c:
            first = lay_first_weights(nc, c)
            with nc.sbuf_tensor("pad_rec", [P, 16, RW], F32) as pad_rec:
                spent = phase_node_tables(kit, first, pad_rec)
                with nc.Block() as block:
                    @block.gpsimd
                    def _(pool):
                        for spent_sem in spent:
                            pool.sem_clear(spent_sem)
                phase_sort(kit, pad_rec, records_clear)
            with ExitStack() as c2:
                acc = c2.enter_context(nc.sbuf_tensor("flow_sum", [P, BINS, D], F32))
                phase_first_edges(kit, first, acc, rec_in, rows_in)
                phase_first_nodes(kit, first, acc)
        with ExitStack() as c:
            acc = c.enter_context(nc.sbuf_tensor("mix_sum", [P, NBLK, QW], F32))
            phase_second_edges(kit, acc, rec_in, rows_in)
            phase_second_nodes(kit, acc)


ROWS = ["d2t_b2", "t2d_b2", "d2t_g2", "t2d_g2", "d2t_be2", "t2d_be2", "node_b", "self_b", "node_g", "self_g",
        "node_be", "self_be"]
B2, G2, BE2, NSB, NSG, NSBE = 0, 2, 4, 6, 8, 10


def lay_first_weights(nc, ctx):
    def sb(name, shape):
        return ctx.enter_context(nc.sbuf_tensor(name, shape, F32))

    return {
        "w1x": sb("w1x", [P, 2, H]),
        "w1e": sb("w1e", [EA + 1, 2, H]),
        "w2": sb("w2", [P, 2, 2, D]),
        "gb1": sb("gb1", [P, 2, 4]),
        "rows": sb("rows", [P, 12, D]),
        "nsw": sb("nsw", [P, 3, D]),
        "watt": sb("watt", [P, 2]),
        "batt": sb("batt", [P, 1]),
    }


def phase_node_tables(kit, w, pad_rec):
    nc, t, out, dram, woken, x_s, ident, iota_f, eps_s, zero_s, tab_s = kit
    spent = []
    with ExitStack() as ctx:
        def sb(name, shape, dt=F32):
            return ctx.enter_context(nc.sbuf_tensor("a_" + name, shape, dt))

        def ps(name, shape):
            return ctx.enter_context(nc.psum_tensor("a_" + name, shape, F32))

        def sem(name):
            spent.append(ctx.enter_context(nc.semaphore(name)))
            return spent[-1]

        means = sb("means", [P, 32])
        xc = sb("xc", [P, 4, D])
        xt = sb("xt", [P, 4, D])
        u_out = sb("u_out", [P, 4, 2 * H])
        ab_s = sb("ab_s", [P, NBLK, 2])
        p_t = [ps(f"p_t{i}", [P, 512]) for i in range(2)]
        p_u = [ps(f"p_u{i}", [P, 512]) for i in range(2)]
        p_ab = [ps(f"p_ab{i}", [P, 512]) for i in range(2)]
        loaded, cleared, constants = sem("a_loaded"), sem("a_cleared"), sem("a_constants")
        dve_chain, pool_chain, centred = sem("a_dve_chain"), sem("a_pool_chain"), sem("a_centred")
        x_staged, x_turned, xt_ready = sem("a_x_staged"), sem("a_x_turned"), sem("a_xt_ready")
        u_made, u_ready = sem("a_u_made"), sem("a_u_ready")
        u_stored = [sem(f"a_u_stored{i}") for i in range(4)]
        stored = sem("a_stored")
        loads = []

        def load(dst, src):
            loads.append((dst, src))

        load(x_s[:, 0:NBLK - 1, :], t["x"][0:(NBLK - 1) * P, :].rearrange("(b p) f -> p b f", p=P))
        load(x_s[0:NLAST, NBLK - 1, :], t["x"][(NBLK - 1) * P:N, :])
        for d, pre in enumerate(("L0_gnn_d2t_", "L0_gnn_t2d_")):
            load(w["w1x"][:, d, :], t[pre + "w1"][0:D, :])
            load(w["w1e"][0:EA, d, :], t[pre + "w1"][D:D + EA, :])
            load(w["w1e"][EA:EA + 1, d, :], t[pre + "b1"].unsqueeze(0))
            load(w["w2"][:, d, :, :], t[pre + "w2"].rearrange("(c k) f -> k c f", c=2))
            load(w["gb1"][:, d, 0:2], t[pre + "g1"].rearrange("(c k) -> k c", c=2))
            load(w["gb1"][:, d, 2:4], t[pre + "be1"].rearrange("(c k) -> k c", c=2))
        for i, name in enumerate(ROWS):
            load(w["rows"][:, i, :], t["L0_gnn_" + name].partition_broadcast(P))
        load(w["nsw"][:, 0:2, :], t["L0_gnn_node_w"].rearrange("(c k) f -> k c f", c=2))
        load(w["nsw"][:, 2, :], t["L0_gnn_self_w"])
        load(w["watt"][:, :], t["L0_gnn_w_att"].rearrange("(c k) o -> k (c o)", c=2))
        load(w["batt"][:, :], t["L0_gnn_b_att"].partition_broadcast(P))

        block = ctx.enter_context(nc.Block())

        @block.sync
        def _(sp):
            engine = Waits(sp, woken["sp"])
            engine.wait_ge(cleared, 2)
            for dst, src in loads:
                sp.dma_start(dst, src).then_inc(loaded, 16)
            def store(s):
                r = s.slot(4)
                engine.wait_ge(u_ready, s.n(1, 1))
                sp.dma_start(dram["u"].rearrange("(d n) f -> n d f", d=2)[bass.ds(s.n(P), P), :, :],
                             u_out[:, r, :].rearrange("p (d f) -> p d f", d=2)).then_inc(u_stored[r], 16)

            pipeline(sp, NBLK, 4, [(0, store)])
            for i in range(2):
                sp.dma_start((dram["a"], dram["b"])[i].rearrange("(b p) o -> p (b o)", p=P),
                             ab_s[:, :, i]).then_inc(stored, 16)
            engine.wait_ge(stored, 32)
            for r in range(4):
                engine.wait_ge(u_stored[r], 16 * len(range(r, NBLK, 4)))

        @block.gpsimd
        def _(pool):
            nc.gpsimd.memset(ident[:, :], 0.0).then_inc(pool_chain, 1)
            pool.wait_ge(pool_chain, 1)
            nc.gpsimd.affine_select(out=ident[:, :], in_=ident[:, :], compare_op=ALU.not_equal, fill=1.0, base=0,
                                    pattern=[[-1, P]], channel_multiplier=1).then_inc(constants, 1)
            nc.gpsimd.iota(iota_f[:, :], [[1, P]], base=0, channel_multiplier=0,
                           allow_small_or_imprecise_dtypes=True).then_inc(constants, 1)

        @block.vector
        def _(dve):
            engine = Waits(dve, woken["dve"])
            count = [0]

            def link(ins):
                count[0] += 1
                ins.then_inc(dve_chain, 1)
                dve.wait_ge(dve_chain, count[0])

            nc.vector.memset(x_s[:, NBLK - 1, :], 0.0).then_inc(cleared, 1)
            link(nc.vector.memset(pad_rec[:, :, :], 0.0))
            nc.vector.memset(pad_rec[:, :, R_LOC1:R_LOC0 + 1], -1.0).then_inc(cleared, 1)
            nc.vector.memset(zero_s[:, :], 0.0).then_inc(constants, 1)
            nc.vector.memset(eps_s[:, :], LN_EPS).then_inc(constants, 1)
            dve.wait_ge(loaded, 16 * len(loads))
            centre = [(w["w1x"][:, d, :], P, H) for d in range(2)]
            centre += [(w["w1e"][:, d, :], EA + 1, H) for d in range(2)]
            centre += [(w["w2"][:, d, c, :], P, D) for d in range(2) for c in range(2)]
            centre += [(w["rows"][:, i, :], P, D) for i in (B2, B2 + 1, NSB, NSB + 1)]
            centre += [(w["nsw"][:, i, :], P, D) for i in range(3)]
            for i, (ap, rows, width) in enumerate(centre):
                last = nc.vector.reduce_sum(means[0:rows, i:i + 1], ap, axis=AX_X)
            link(last)
            for i, (ap, rows, width) in enumerate(centre):
                last = nc.vector.tensor_scalar(means[0:rows, i:i + 1], means[0:rows, i:i + 1], -1.0 / width, None,
                                               ALU.mult)
            link(last)
            for i, (ap, rows, width) in enumerate(centre):
                last = nc.vector.tensor_scalar(ap, ap, means[0:rows, i:i + 1], None, ALU.add)
            last.then_inc(centred, 1)

            def evacuate(s):
                r, h = s.slot(4), s.slot(2)
                engine.wait_ge(u_made, s.n(1, 1))
                engine.wait_ge(u_stored[r], s.turn(4, 16))
                nc.vector.tensor_copy(ab_s[:, bass.ds(s.n(), 1), :], p_ab[h][:, 0:2].unsqueeze(1))
                nc.vector.tensor_copy(u_out[:, r, :], p_u[h][:, :]).then_inc(u_ready, 1)

            pipeline(dve, NBLK, 4, [(0, evacuate)])

        @block.scalar
        def _(act):
            engine = Waits(act, woken["act"])
            act.wait_ge(loaded, 16 * len(loads))

            def stage_x(s):
                if s.trip is not None or s.at >= 4:
                    engine.wait_ge(x_turned, s.n(1, -3))
                nc.scalar.copy(xc[:, s.slot(4), :].unsqueeze(1),
                               x_s[:, bass.ds(s.n(), 1), 0:D]).then_inc(x_staged, 1)

            def copy_xt(s):
                engine.wait_ge(x_turned, s.n(1, 1))
                if s.trip is not None or s.at >= 4:
                    engine.wait_ge(u_made, s.n(1, -3))
                nc.scalar.copy(xt[:, s.slot(4), :], p_t[s.slot(2)][:, 0:P]).then_inc(xt_ready, 1)

            pipeline(act, NBLK, 4, [(1, copy_xt), (0, stage_x)])

        @block.tensor
        def _(pe):
            engine = Waits(pe, woken["pe"])
            pe.wait_ge(constants, 4)
            pe.wait_ge(centred, 1)

            def turn(s):
                engine.wait_ge(x_staged, s.n(1, 1))
                if s.trip is not None or s.at >= 2:
                    engine.wait_ge(xt_ready, s.n(1, -1))
                nc.tensor.transpose(p_t[s.slot(2)][:, 0:P], xc[:, s.slot(4), :], ident[:, :]).then_inc(x_turned, 1)

            def product(s):
                h = s.slot(2)
                engine.wait_ge(xt_ready, s.n(1, 1))
                if s.trip is not None or s.at >= 2:
                    engine.wait_ge(u_ready, s.n(1, -1))
                xtb = xt[:, s.slot(4), :]
                nc.tensor.matmul(p_ab[h][:, 0:2], xtb, w["watt"][:, :], start=True, stop=True)
                nc.tensor.matmul(p_u[h][:, :], xtb, w["w1x"][:, :, :].rearrange("p d f -> p (d f)"), start=True,
                                 stop=True).then_inc(u_made, 1)

            pipeline(pe, NBLK, 4, [(1, product), (0, turn)])
    return spent


def phase_sort(kit, pad_rec, records_clear):
    nc, t, out, dram, woken, x_s, ident, iota_f, eps_s, zero_s, tab_s = kit
    LOT = 5
    LOTS = ET // LOT
    with ExitStack() as ctx:
        def sb(name, shape, dt=F32):
            return ctx.enter_context(nc.sbuf_tensor("b_" + name, shape, dt))

        def ps(name, shape):
            return ctx.enter_context(nc.psum_tensor("b_" + name, shape, F32))

        def sem(name):
            return ctx.enter_context(nc.semaphore(name))

        row_i, col_i = sb("row_i", [EP, ET], I32), sb("col_i", [EP, ET], I32)
        blk_i, loc_i = sb("blk_i", [EP, ET], I32), sb("loc_i", [EP, ET], I32)
        row_f, col_f = sb("row_f", [EP, ET]), sb("col_f", [EP, ET])
        up, down = sb("up", [EP, ET]), sb("down", [EP, ET])
        bin_f = sb("bin_f", [EP, ET])
        tail = sb("tail", [EP, ET, RW - EA])
        ea4_s = sb("ea4_s", [EP, ET, 4])
        from_col, from_row = sb("from_col", [EP, ET]), sb("from_row", [EP, ET])
        slot_f, slot_i = sb("slot_f", [EP, ET]), sb("slot_i", [EP, ET], I32)
        tmp = sb("tmp", [EP, 2, ET])
        lim = sb("lim", [EP, 2, ET])
        junk = sb("junk", [P, 2, ET], BF16)
        count_s = sb("count_s", [EP, BINS])
        held = sb("held", [EP, 2, BINS])
        junk2 = sb("junk2", [EP, 2, BINS])
        lower = sb("lower", [EP, EP])
        ones = sb("ones", [P, P])
        size_i, size_f = sb("size_i", [P, BINS], I32), sb("size_f", [P, BINS])
        ends, starts = sb("ends", [P, BINS]), sb("starts", [P, BINS])
        gstart = sb("gstart", [P, GROUPS // P])
        tab_f = sb("tab_f", [P, 3, GROUPS // P])
        tab_i = sb("tab_i", [P, 3, GROUPS // P], I32)
        stats = sb("stats", [P, 8])
        batt = sb("batt_s", [EP, 1])
        icol, gcol = sb("icol", [EP, 2, LOT], I32), sb("gcol", [EP, 2, LOT])
        stage = sb("stage", [EP, 4, LOT, RW])
        islot = sb("islot", [EP, 4, LOT], I32)
        hl_b = sb("hl_b", [EP, 2, ET], BF16)
        hl_pad = sb("hl_pad", [1, CHUNKS * CHUNK - E], BF16)
        line_hi = sb("line_hi", [NBLK, 2, LINE * CHUNK], BF16)
        line_lo = sb("line_lo", [P, 2, LINE * CHUNK], BF16)
        lane = sb("lane", [P, 1])
        table = sb("row_table", [NBLK, 3, P])
        table_b = sb("row_table_b", [NBLK, 3, P], BF16)
        of_block = sb("of_block", [NBLK, 2, CHUNK], BF16)
        masked = sb("masked", [P, 2, CHUNK])
        found = sb("found", [P, 7, P])
        found_t = sb("found_t", [P, 7, P])
        p_low = ps("p_low", [P, 512])
        p_all = p_low[:, BINS:2 * BINS]
        p_r = ps("p_r", [P, 512])
        p_tb = [ps(f"p_tb{i}", [P, 512]) for i in range(2)]

        loaded, ready = sem("b_loaded"), sem("b_ready")
        dve_chain, pool_chain = sem("b_dve_chain"), sem("b_pool_chain")
        i_staged = sem("b_i_staged")
        gathered = [sem(f"b_gathered{i}") for i in range(2)]
        logits_in = sem("b_logits_in")
        hist_done, hist_summed = sem("b_hist_done"), sem("b_hist_summed")
        held_step, hist_step = sem("b_held_step"), sem("b_hist_step")
        tab_ready, tab_out, tab_in = sem("b_tab_ready"), sem("b_tab_out"), sem("b_tab_in")
        max_part, max_all, exp_done = sem("b_max_part"), sem("b_max_all"), sem("b_exp_done")
        sum_all, tail_ready = sem("b_sum_all"), sem("b_tail_ready")
        max_negated = sem("b_max_negated")
        hl_ready, hl_out, table_in, table_ready = sem("l_hl_ready"), sem("l_hl_out"), sem("l_table_in"), sem("l_table")
        line_in = [sem(f"l_line_in{i}") for i in range(2)]
        block_found = sem("l_block_found")
        looked_up, masked_ready, picked, kept = sem("l_looked_up"), sem("l_masked"), sem("l_picked"), sem("l_kept")
        turned, turned_out, found_out, row_in = sem("l_turned"), sem("l_turned_out"), sem("l_found_out"), sem("l_row_in")

        with nc.Block() as block:
            @block.sync
            def _(sp):
                engine = Waits(sp, woken["sp"])
                for lo, hi in split(EP):
                    for dst, src in ((row_i, t["src"]), (col_i, t["dst"])):
                        sp.dma_start(dst[lo:hi, :], src.rearrange("(p t) -> p t", p=EP)[lo:hi, :]).then_inc(loaded, 16)
                for lo, hi in split(EP):
                    sp.dma_start(ea4_s[lo:hi, :, :], t["edge_attr_4"].rearrange("(p t) w -> p t w", p=EP)[lo:hi, :, :])\
                        .then_inc(loaded, 16)
                sp.dma_start(batt[:, :], t["L0_gnn_b_att"].partition_broadcast(EP)).then_inc(loaded, 16)
                sp.wait_ge(loaded, 16 * 7)
                slots = dram["rec"].rearrange("(p q r) w -> p q (r w)", p=P, r=16)
                pads = pad_rec[:, :, :].rearrange("p r w -> p (r w)").unsqueeze(1)
                now = GROUPS * SLOTS // (16 * P) - CHUNKS // LINE
                sp.dma_start(slots[:, 0:now, :], pads.to_broadcast([P, now, 16 * RW])).then_inc(records_clear, 16)
                sp.dma_start(table[:, 0, :], dram["b"].rearrange("(b p) o -> b (p o)", p=P)).then_inc(table_in, 16)
                engine.wait_ge(hl_ready, 2)
                for i in range(2):
                    sp.dma_start(dram["rows"][i, 0:E].rearrange("(p t) -> p t", p=EP), hl_b[:, i, :])\
                        .then_inc(hl_out, 16)
                    sp.dma_start(dram["rows"][i:i + 1, E:CHUNKS * CHUNK], hl_pad[:, :]).then_inc(hl_out, 16)
                engine.wait_ge(tab_ready, 1)
                sp.dma_start(dram["tab"].rearrange("c (s p) -> p c s", p=P), tab_i[:, :, :]).then_inc(tab_out, 16)
                engine.wait_ge(tab_out, 16)
                sp.dma_start(tab_s[:, :, :], dram["tab"].unsqueeze(0)).then_inc(tab_in, 16)
                engine.wait_ge(tab_in, 16)
                engine.wait_ge(hl_out, 64)

                def load_line(s):
                    r = s.slot(2)
                    if s.trip is not None or s.at >= 2:
                        engine.wait_ge(masked_ready, s.n(LINE, -LINE))
                    for i, (dst, rows) in enumerate(((line_hi, NBLK), (line_lo, P))):
                        sp.dma_start(dst[:, r, :], dram["rows"][i, bass.ds(s.n(LINE * CHUNK), LINE * CHUNK)]
                                     .partition_broadcast(rows)).then_inc(line_in[r], 16)
                    sp.dma_start(slots[:, bass.ds(s.n(1, now), 1), :], pads).then_inc(records_clear, 16)

                pipeline(sp, CHUNKS // LINE, 2, [(0, load_line)])
                tiles = CHUNKS * CHUNK // P
                engine.wait_ge(turned_out, 2)
                sp.dma_start(dram["from_row"][0:6 * P * P, :].rearrange("(q c e) o -> c q (e o)", q=6, c=P),
                             found_t[:, 0:6, :]).then_inc(found_out, 16)
                sp.dma_start(dram["from_row"][6 * P * P:, :].rearrange("(c e) o -> c (e o)", e=P),
                             found_t[0:tiles - 6 * P, 6, :]).then_inc(found_out, 16)
                engine.wait_ge(found_out, 32)
                for lo, hi in split(EP):
                    sp.dma_start(from_row[lo:hi, :], dram["from_row"][0:E, :].rearrange("(p t) o -> p (t o)", p=EP)
                                 [lo:hi, :]).then_inc(row_in, 16)
                engine.wait_ge(row_in, 32)

            @block.gpsimd
            def _(pool):
                engine = Waits(pool, woken["pool"])
                nc.gpsimd.memset(lower[:, :], 1.0).then_inc(pool_chain, 1)
                pool.wait_ge(pool_chain, 1)
                nc.gpsimd.affine_select(out=lower[:, :], in_=lower[:, :], compare_op=ALU.is_gt, fill=0.0, base=0,
                                        pattern=[[1, EP]], channel_multiplier=-1).then_inc(ready, 1)
                nc.gpsimd.iota(gstart[:, :], [[P, GROUPS // P]], base=0, channel_multiplier=1,
                               allow_small_or_imprecise_dtypes=True).then_inc(ready, 1)
                nc.gpsimd.iota(lane[:, :], [[1, 1]], base=0, channel_multiplier=1,
                               allow_small_or_imprecise_dtypes=True).then_inc(ready, 1)

                def gather(s):
                    h = s.slot(2)
                    engine.wait_ge(i_staged, s.n(1, 1))
                    for j in range(LOT):
                        nc.gpsimd.indirect_dma_start(
                            gcol[:, h, j:j + 1], None, dram["a"],
                            bass.IndirectOffsetOnAxis(ap=icol[:, h, j:j + 1], axis=0)).then_inc(gathered[h], 16)

                pipeline(pool, LOTS, 2, [(0, gather)])
                pool.wait_ge(max_part, 1)
                nc.gpsimd.partition_all_reduce(stats[:, 2:4], stats[:, 0:2], P, RMAX).then_inc(max_all, 1)
                pool.wait_ge(exp_done, 2)
                nc.gpsimd.partition_all_reduce(stats[:, 6:8], stats[:, 4:6], P, RADD).then_inc(sum_all, 1)

            @block.scalar
            def _(act):
                engine = Waits(act, woken["act"])
                act.wait_ge(loaded, 16 * 7)

                def take(s):
                    h = s.slot(2)
                    engine.wait_ge(gathered[h], s.turn(2, 16 * LOT, 16 * LOT))
                    nc.scalar.copy(from_col[:, bass.ds(s.n(LOT), LOT)], gcol[:, h, :]).then_inc(logits_in, 1)

                def give(s):
                    h = s.slot(2)
                    if s.trip is not None or s.at >= 2:
                        engine.wait_ge(logits_in, s.n(1, -1))
                    nc.scalar.copy(icol[:, h, :], col_i[:, bass.ds(s.n(LOT), LOT)]).then_inc(i_staged, 1)

                pipeline(act, LOTS, 2, [(2, take), (0, give)])
                act.wait_ge(max_negated, 1)
                for d in range(2):
                    nc.scalar.activation(tmp[:, d, :], lim[:, d, :], ACT.Exp, bias=stats[0:EP, 2 + d:3 + d],
                                         accum_out=stats[0:EP, 4 + d:5 + d]).then_inc(exp_done, 1)

            @block.tensor
            def _(pe):
                engine = Waits(pe, woken["pe"])
                pe.wait_ge(ready, 4)
                pe.wait_ge(hist_done, 1)
                nc.tensor.matmul(p_low[0:EP, 0:BINS], lower[:, :], count_s[:, :], start=True, stop=True)
                nc.tensor.matmul(p_all, ones[0:EP, :], count_s[:, :], start=True, stop=True).then_inc(hist_summed, 1)
                pe.wait_ge(table_ready, 1)

                def look_up(s):
                    h = s.slot(2)
                    engine.wait_ge(block_found, s.n(1, 1))
                    if s.trip is not None or s.at >= 2:
                        engine.wait_ge(masked_ready, s.n(1, -1))
                    for i in range(3):
                        last = nc.tensor.matmul(p_tb[h][:, :], table_b[:, i, :], of_block[:, h, :], start=(i == 0),
                                                stop=(i == 2))
                    last.then_inc(looked_up, 1)

                def pick(s):
                    h = s.slot(2)
                    engine.wait_ge(masked_ready, s.n(1, 1))
                    if s.slot(8) == 0 and (s.trip is not None or s.at >= 8):
                        engine.wait_ge(kept, s.turn(8, 8))
                    for i in range(CHUNK // P):
                        last = nc.tensor.matmul(p_r[:, s.slot(8) * 4 + i:s.slot(8) * 4 + i + 1],
                                                masked[:, h, i * P:(i + 1) * P], ones[:, 0:1], start=True, stop=True)
                    last.then_inc(picked, 1)

                pipeline(pe, CHUNKS, 8, [(1, look_up), (3, pick)])
                engine.wait_ge(kept, CHUNKS + 1)
                for q in range(7):
                    p = p_tb[0] if q < 4 else p_tb[1]
                    last = nc.tensor.transpose(p[:, q % 4 * P:(q % 4 + 1) * P], found[:, q, :], ident[:, :])
                    if q in (3, 6):
                        last.then_inc(turned, 1)

            @block.vector
            def _(dve):
                engine = Waits(dve, woken["dve"])
                count = [0]

                def link(ins):
                    count[0] += 1
                    ins.then_inc(dve_chain, 1)
                    dve.wait_ge(dve_chain, count[0])

                V = nc.vector
                V.memset(ones[:, :], 1.0).then_inc(ready, 1)
                V.memset(found[:, :, :], 0.0)
                V.memset(hl_pad[:, :], 0.0).then_inc(hl_ready, 1)
                V.memset(stats[:, 0:2], -BIG)
                link(V.memset(stats[:, 4:6], 0.0))
                dve.wait_ge(loaded, 16 * 7)
                V.tensor_copy(row_f[:, :], row_i[:, :])
                V.tensor_copy(col_f[:, :], col_i[:, :])
                V.tensor_single_scalar(blk_i[:, :], row_i[:, :], 7, ALU.logical_shift_right)
                link(V.tensor_single_scalar(loc_i[:, :], row_i[:, :], P - 1, ALU.bitwise_and))
                V.tensor_copy(bin_f[:, :], blk_i[:, :])
                V.tensor_copy(hl_b[:, 0, :], blk_i[:, :])
                V.tensor_copy(hl_b[:, 1, :], loc_i[:, :]).then_inc(hl_ready, 1)
                dve.wait_ge(table_in, 16)
                for i in range(3):
                    link(V.tensor_copy(table_b[:, i, :], table[:, i, :]))
                    if i < 2:
                        link(V.tensor_tensor(table[:, i + 1, :], table[:, i, :], table_b[:, i, :], ALU.subtract))
                V.memset(junk[:, 0, 0:1], 0.0).then_inc(table_ready, 1)
                V.tensor_copy(tail[:, :, R_LOC1 - EA], loc_i[:, :])
                V.tensor_tensor(up[:, :], row_f[:, :], col_f[:, :], ALU.is_lt)
                V.tensor_tensor(down[:, :], row_f[:, :], col_f[:, :], ALU.is_gt)
                link(V.tensor_copy(tail[:, :, 0:4], ea4_s[:, :, :]))
                V.scalar_tensor_tensor(out=bin_f[:, :], in0=down[:, :], scalar=float(NBLK), in1=bin_f[:, :],
                                       op0=ALU.mult, op1=ALU.add)
                V.scalar_tensor_tensor(out=tail[:, :, R_COL - EA], in0=down[:, :], scalar=float(NPAD),
                                       in1=col_f[:, :], op0=ALU.mult, op1=ALU.add)
                link(V.tensor_tensor(tmp[:, 0, :], up[:, :], down[:, :], ALU.add))
                link(V.scalar_tensor_tensor(out=tmp[:, 1, :], in0=tail[:, :, R_LOC1 - EA], scalar=1.0,
                                            in1=tmp[:, 0, :], op0=ALU.add, op1=ALU.mult))
                link(V.tensor_scalar(tail[:, :, R_LOC0 - EA], tmp[:, 1, :], -1.0, None, ALU.add))
                def count_bin(s):
                    if s.trip is not None or s.at >= 2:
                        engine.wait_ge(hist_step, s.n(1, -1))
                    V.tensor_scalar(junk[0:EP, s.slot(2), :], bin_f[:, :], iota_f[0:EP, bass.ds(s.n(), 1)], None,
                                    ALU.is_equal, ALU.add, accum_out=count_s[:, bass.ds(s.n(), 1)])\
                        .then_inc(hist_step, 1)

                pipeline(dve, BINS, 2, [(0, count_bin)])
                dve.wait_ge(hist_step, BINS)
                V.memset(junk2[:, :, :], 0.0).then_inc(hist_done, 1)
                dve.wait_ge(hist_summed, 1)
                link(V.tensor_scalar(size_i[:, :], p_all, float(SLOTS - 1), None, ALU.add))
                link(V.tensor_scalar(size_i[:, :], size_i[:, :], 8, 8, ALU.logical_shift_right,
                                     ALU.logical_shift_left))
                link(V.tensor_copy(size_f[:, :], size_i[:, :]))
                link(V.tensor_tensor_scan(ends[:, :], ones[:, 0:BINS], size_f[:, :], 0.0, ALU.mult, ALU.add))
                link(V.tensor_tensor(starts[:, :], ends[:, :], size_f[:, :], ALU.subtract))
                V.tensor_tensor(held[:, 0, :], starts[0:EP, :], p_low[0:EP, 0:BINS], ALU.add).then_inc(held_step, 1)
                link(V.tensor_scalar(gstart[:, :], gstart[:, :], float(SLOTS), None, ALU.mult))
                for s in range(GROUPS // P):
                    last = V.tensor_scalar(junk[:, 0, BINS * s:BINS * (s + 1)], ends[:, :], gstart[:, s:s + 1], None, ALU.is_le, ALU.add,
                                           accum_out=tab_f[:, 0, s:s + 1])
                link(last)
                link(V.tensor_scalar(tab_f[:, 0, :], tab_f[:, 0, :], float(BINS - 1), None, ALU.min))
                link(V.tensor_scalar(tab_f[:, 1, :], tab_f[:, 0, :], float(NBLK), None, ALU.is_ge))
                link(V.scalar_tensor_tensor(out=tab_f[:, 2, :], in0=tab_f[:, 1, :], scalar=-float(NBLK),
                                            in1=tab_f[:, 0, :], op0=ALU.mult, op1=ALU.add))
                V.tensor_copy(tab_i[:, :, :], tab_f[:, :, :]).then_inc(tab_ready, 1)

                def place(tile, h):
                    engine.wait_ge(held_step, tile + 1)
                    V.scalar_tensor_tensor(out=junk2[:, h, :], in0=iota_f[0:EP, 0:BINS],
                                           scalar=bin_f[:, bass.ds(tile, 1)], in1=held[:, h, :],
                                           op0=ALU.is_equal, op1=ALU.mult, accum_out=slot_f[:, bass.ds(tile, 1)])
                    V.scalar_tensor_tensor(out=held[:, 1 - h, :], in0=iota_f[0:EP, 0:BINS],
                                           scalar=bin_f[:, bass.ds(tile, 1)], in1=held[:, h, :],
                                           op0=ALU.is_equal, op1=ALU.add).then_inc(held_step, 1)

                def place_two(s, q):
                    for k in range(2):
                        place(s.n(PER_CHUNK, 2 * q + k), k)

                def find_block(s):
                    r, at = s.slot(2 * LINE) // LINE, s.slot(LINE) * CHUNK
                    if s.slot(LINE) == 0:
                        engine.wait_ge(line_in[r], s.turn(2 * LINE, 32, 32))
                    V.tensor_scalar(of_block[:, s.slot(2), :], line_hi[:, r, at:at + CHUNK], lane[0:NBLK, :], None, ALU.is_equal)\
                        .then_inc(block_found, 1)

                def mask(s):
                    r, h, at = s.slot(2 * LINE) // LINE, s.slot(2), s.slot(LINE) * CHUNK
                    engine.wait_ge(looked_up, s.n(1, 1))
                    if s.trip is not None or s.at >= 2:
                        engine.wait_ge(picked, s.n(1, -1))
                    V.scalar_tensor_tensor(out=masked[:, h, :], in0=line_lo[:, r, at:at + CHUNK], scalar=lane[:, :],
                                           in1=p_tb[h][:, :], op0=ALU.is_equal, op1=ALU.mult).then_inc(masked_ready, 1)

                def keep(s):
                    if s.slot(8) == 7:
                        engine.wait_ge(picked, s.n(1, 1))
                        V.tensor_copy(found.rearrange("p q c -> p (q c)")[:, bass.ds(s.n(4, -28), 32)], p_r[:, 0:32])\
                            .then_inc(kept, 8)

                pipeline(dve, CHUNKS, 8, [(4, keep), (2, mask), (0, lambda s: place_two(s, 0)), (0, find_block),
                                          (0, lambda s: place_two(s, 1))])
                for tile in range(CHUNKS * PER_CHUNK, ET):
                    place(tile, tile % 2)
                dve.wait_ge(held_step, ET + 1)
                V.tensor_copy(slot_i[:, :], slot_f[:, :])
                V.memset(junk[:, 0, 0:1], 0.0).then_inc(kept, 1)
                for q in range(2):
                    dve.wait_ge(turned, q + 1)
                    n = (4, 3)[q]
                    V.tensor_copy(found_t[:, 4 * q:4 * q + n, :].rearrange("p q c -> p (q c)"), p_tb[q][:, 0:n * P])\
                        .then_inc(turned_out, 1)
                dve.wait_ge(logits_in, LOTS)
                dve.wait_ge(row_in, 32)
                link(V.tensor_tensor(from_col[:, :], from_col[:, :], from_row[:, :], ALU.add))
                link(V.tensor_scalar(from_col[:, :], from_col[:, :], batt[:, :], None, ALU.add))
                link(V.scalar_tensor_tensor(out=from_row[:, :], in0=from_col[:, :], scalar=SLOPE, in1=from_col[:, :],
                                            op0=ALU.mult, op1=ALU.max))
                V.tensor_scalar(lim[:, 0, :], up[:, :], 2 * BIG, -BIG, ALU.mult, ALU.add)
                link(V.tensor_scalar(lim[:, 1, :], down[:, :], 2 * BIG, -BIG, ALU.mult, ALU.add))
                for d in range(2):
                    last = V.tensor_tensor(lim[:, d, :], lim[:, d, :], from_row[:, :], ALU.min)
                link(last)
                for d in range(2):
                    last = V.reduce_max(stats[0:EP, d:d + 1], lim[:, d, :], axis=AX_X)
                last.then_inc(max_part, 1)
                dve.wait_ge(max_all, 1)
                V.tensor_scalar(stats[:, 2:4], stats[:, 2:4], -1.0, None, ALU.mult).then_inc(max_negated, 1)
                dve.wait_ge(exp_done, 2)
                V.tensor_tensor(tmp[:, 0, :], tmp[:, 0, :], up[:, :], ALU.mult)
                V.tensor_tensor(tmp[:, 1, :], tmp[:, 1, :], down[:, :], ALU.mult)
                dve.wait_ge(sum_all, 1)
                link(V.reciprocal(stats[:, 6:8], stats[:, 6:8]))
                link(V.tensor_scalar(tmp[:, 0, :], tmp[:, 0, :], stats[0:EP, 6:7], None, ALU.mult))
                V.scalar_tensor_tensor(out=tail[:, :, R_ATT - EA], in0=tmp[:, 1, :], scalar=stats[0:EP, 7:8],
                                       in1=tmp[:, 0, :], op0=ALU.mult, op1=ALU.add).then_inc(tail_ready, 1)

        features_in = [sem(f"s_features_in{i}") for i in range(4)]
        staged = sem("s_staged")
        scattered = [sem(f"s_scattered{i}") for i in range(4)]
        with nc.Block() as block:
            @block.sync
            def _(sp):
                engine = Waits(sp, woken["sp"])

                def features(s):
                    r = s.slot(4)
                    engine.wait_ge(scattered[r], s.turn(4, 16 * LOT))
                    for lo, hi in split(EP):
                        sp.dma_start(stage[lo:hi, r, :, 0:EA],
                                     t["edge_attr_64"].rearrange("(p t) w -> p t w", p=EP)
                                     [lo:hi, bass.ds(s.n(LOT), LOT), :]).then_inc(features_in[r], 16)

                pipeline(sp, LOTS, 4, [(0, features)])

            @block.vector
            def _(dve):
                engine = Waits(dve, woken["dve"])

                def tails(s):
                    r = s.slot(4)
                    engine.wait_ge(scattered[r], s.turn(4, 16 * LOT))
                    nc.vector.tensor_copy(stage[:, r, :, EA:RW], tail[:, bass.ds(s.n(LOT), LOT), :])
                    nc.vector.tensor_copy(islot[:, r, :], slot_i[:, bass.ds(s.n(LOT), LOT)]).then_inc(staged, 1)

                pipeline(dve, LOTS, 4, [(0, tails)])

            @block.gpsimd
            def _(pool):
                engine = Waits(pool, woken["pool"])

                pool.wait_ge(records_clear, 16 * (1 + CHUNKS // LINE))

                def scatter(s):
                    r = s.slot(4)
                    engine.wait_ge(staged, s.n(1, 1))
                    engine.wait_ge(features_in[r], s.turn(4, 32, 32))
                    for j in range(LOT):
                        nc.gpsimd.indirect_dma_start(
                            dram["rec"], bass.IndirectOffsetOnAxis(ap=islot[:, r, j:j + 1], axis=0),
                            stage[:, r, j, :], None).then_inc(scattered[r], 16)

                pipeline(pool, LOTS, 4, [(0, scatter)])
                for r in range(4):
                    engine.wait_ge(scattered[r], 16 * LOT * len(range(r, LOTS, 4)))


def phase_first_edges(kit, w, acc, rec_in, u_in):
    nc, t, out, dram, woken, x_s, ident, iota_f, eps_s, zero_s, tab_s = kit
    T = TPG * PAIR
    STEPS = GROUPS // PAIR
    with ExitStack() as ctx:
        def sb(name, shape, dt=F32):
            return ctx.enter_context(nc.sbuf_tensor("e_" + name, shape, dt))

        def ps(name, cols=512):
            return ctx.enter_context(nc.psum_tensor("e_" + name, [P, cols], F32))

        def sem(name):
            return ctx.enter_context(nc.semaphore(name))

        rec = sb("rec", [P, RING, T, RW])
        index = sb("index", [P, RING, T], I32)
        u = sb("u", [P, RING, T, H])
        onehot = sb("onehot", [P, AHEAD, T, P])
        ea1 = sb("ea1", [P, RING, T, EA + 1])
        ea1_t = sb("ea1_t", [EA + 1, 2, T * P])
        v = sb("v", [P, RING, T, H])
        vn = sb("vn", [P, RING, T, H])
        h_t = sb("h_t", [P, 2, 2, T * P])
        v2 = sb("v2", [P, 2, T, D])
        h2 = sb("h2", [P, 2, T, D])
        junk = sb("junk", [P, 2, T, H])
        sq, dev, inv = sb("sq", [P, 2, 2, T]), sb("dev", [P, 2, 2, T]), sb("inv", [P, 2, 2, T])
        p_ea = ps("p_ea")
        p_v = ps("p_v", T * H)
        p_turn = ps("p_turn", 2 * T * P)
        p_v2, p_sum = ps("p_v2"), ps("p_sum")

        onehot_ready, index_ready, ea1_ready = sem("e_onehot_ready"), sem("e_index_ready"), sem("e_ea1_ready")
        ea1_turned, ea1t_ready, v_in_psum = sem("e_ea1_turned"), sem("e_ea1t_ready"), sem("e_v_in_psum")
        v_ready, sq1_done, dev1_ready = sem("e_v_ready"), sem("e_sq1_done"), sem("e_dev1_ready")
        inv1_done, vn_ready, v_turned = sem("e_inv1_done"), sem("e_vn_ready"), sem("e_v_turned")
        ht_ready, v2_in_psum, v2_ready = sem("e_ht_ready"), sem("e_v2_in_psum"), sem("e_v2_ready")
        sq2_done, dev2_ready, norm2 = sem("e_sq2_done"), sem("e_dev2_ready"), sem("e_norm2")
        h2_ready, summed, added = sem("e_h2_ready"), sem("e_summed"), sem("e_added")
        cleared = sem("e_cleared")
        block = ctx.enter_context(nc.Block())

        def group_value(eng, what, s, g, most):
            return eng.value_load(tab_s[0:1, what, bass.ds(s.n(PAIR, g), 1)], min_val=0, max_val=most)

        @block.sync
        def _(sp):
            engine = Waits(sp, woken["sp"])

            def load(s):
                r = s.slot(RING)
                if s.trip is not None or s.at >= RING:
                    engine.wait_ge(v_ready, s.n(1, 1 - RING))
                    engine.wait_ge(onehot_ready, s.n(1, 1 - RING))
                sp.dma_start(rec[:, r, :, :].rearrange("p (g t) w -> p g (t w)", g=PAIR),
                             dram["rec"].rearrange("(g p t) w -> p g (t w)", p=P, t=TPG)
                             [:, bass.ds(s.n(PAIR), PAIR), :]).then_inc(rec_in[r], 16)

            pipeline(sp, STEPS, AHEAD, [(0, load)])

        @block.gpsimd
        def _(pool):
            engine = Waits(pool, woken["pool"])

            def gather(s):
                r = s.slot(RING)
                engine.wait_ge(index_ready, s.n(1, 1))
                for j in range(T):
                    nc.gpsimd.indirect_dma_start(
                        u[:, r, j, :], None, dram["u"],
                        bass.IndirectOffsetOnAxis(ap=index[:, r, j:j + 1], axis=0)).then_inc(u_in[r], 16)

            def compare(s):
                if s.trip is not None or s.at >= AHEAD:
                    engine.wait_ge(summed, s.n(1, 1 - AHEAD))
                for j in range(T):
                    last = nc.gpsimd.tensor_scalar(onehot[:, s.slot(AHEAD), j, :], iota_f[:, :],
                                                   rec[:, s.slot(RING), j, R_LOC0:R_LOC0 + 1], None, ALU.is_equal)
                last.then_inc(onehot_ready, 1)

            pipeline(pool, STEPS, AHEAD, [(0, gather), (2, compare)])

        @block.tensor
        def _(pe):
            engine = Waits(pe, woken["pe"])
            pe.wait_ge(cleared, 2)

            def turn_ea(s):
                r = s.slot(RING)
                engine.wait_ge(ea1_ready, s.n(1, 1))
                if s.trip is not None or s.at >= 1:
                    engine.wait_ge(ea1t_ready, s.n())
                for j in range(T):
                    last = nc.tensor.transpose(p_ea[0:EA + 1, j * P:(j + 1) * P], ea1[:, r, j, :], ident[:, :])
                last.then_inc(ea1_turned, 1)

            def first_product(s):
                h = s.slot(2)
                d = [group_value(pe, 1, s, g, 1) for g in range(PAIR)]
                engine.wait_ge(ea1t_ready, s.n(1, 1))
                if s.trip is not None or s.at >= 1:
                    engine.wait_ge(v_ready, s.n())
                for j in range(T):
                    last = nc.tensor.matmul(p_v[:, j * H:(j + 1) * H], ea1_t[:, h, j * P:(j + 1) * P],
                                            w["w1e"][:, :, :].rearrange("p d f -> p (d f)")
                                            [:, bass.ds(d[j // TPG] * H, H)], start=True, stop=True)
                last.then_inc(v_in_psum, 1)

            def turn_v(s):
                h = s.slot(2)
                engine.wait_ge(vn_ready, s.n(1, 1))
                if s.trip is not None or s.at >= 1:
                    engine.wait_ge(ht_ready, s.n())
                for j in range(T):
                    for c in range(2):
                        last = nc.tensor.transpose(p_turn[:, (c * T + j) * P:(c * T + j + 1) * P],
                                                   vn[:, s.slot(RING), j, c * P:(c + 1) * P], ident[:, :])
                last.then_inc(v_turned, 1)

            def second_product(s):
                h = s.slot(2)
                d = [group_value(pe, 1, s, g, 1) for g in range(PAIR)]
                engine.wait_ge(ht_ready, s.n(1, 1))
                if s.trip is not None or s.at >= 1:
                    engine.wait_ge(v2_ready, s.n())
                w2 = w["w2"][:, :, :, :].rearrange("p d c f -> p (d c f)")
                for j in range(T):
                    for c in range(2):
                        last = nc.tensor.matmul(p_v2[:, j * D:(j + 1) * D], h_t[:, h, c, j * P:(j + 1) * P],
                                                w2[:, bass.ds(d[j // TPG] * H + c * D, D)], start=(c == 0),
                                                stop=(c == 1))
                last.then_inc(v2_in_psum, 1)

            def node_sum(s):
                r, h = s.slot(AHEAD), s.slot(2)
                engine.wait_ge(h2_ready, s.n(1, 1))
                engine.wait_ge(onehot_ready, s.n(1, 1))
                if s.trip is not None or s.at >= 1:
                    engine.wait_ge(added, s.n(PAIR))
                for j in range(T):
                    g, i = divmod(j, TPG)
                    last = nc.tensor.matmul(p_sum[:, g * D:(g + 1) * D], onehot[:, r, j, :], h2[:, h, j, :],
                                            start=(i == 0), stop=(i == TPG - 1))
                last.then_inc(summed, 1)

            pipeline(pe, STEPS, AHEAD, [(2, first_product), (9, node_sum), (6, second_product), (4, turn_v),
                                        (0, turn_ea)])

        @block.scalar
        def _(act):
            engine = Waits(act, woken["act"])
            A = nc.scalar

            def copy_ea(s):
                engine.wait_ge(ea1_turned, s.n(1, 1))
                A.copy(ea1_t[:, s.slot(2), :], p_ea[0:EA + 1, 0:T * P]).then_inc(ea1t_ready, 1)

            def deviation(s, k, source, at, ready, width, squared, made):
                h = s.slot(2)
                engine.wait_ge(ready, s.n(1, 1))
                if s.trip is not None or s.at >= 1:
                    engine.wait_ge(squared, s.n(T))
                for j in range(T):
                    A.activation(junk[:, k, j, 0:width], source[:, at, j, :], ACT.Square, bias=zero_s[:, 0:1],
                                 accum_out=sq[:, h, k, j:j + 1]).then_inc(squared, 1)
                engine.wait_ge(squared, s.n(T, T))
                A.activation(dev[:, h, k, :], sq[:, h, k, :], ACT.Sqrt, bias=eps_s[:, 0:1],
                             scale=1.0 / width).then_inc(made, 1)

            def deviation1(s):
                deviation(s, 0, v, s.slot(RING), v_ready, H, sq1_done, dev1_ready)

            def deviation2(s):
                deviation(s, 1, v2, s.slot(2), v2_ready, D, sq2_done, dev2_ready)

            def relu1(s):
                h = s.slot(2)
                d = [group_value(act, 1, s, g, 1) for g in range(PAIR)]
                engine.wait_ge(v_turned, s.n(1, 1))
                gb1 = w["gb1"][:, :, :].rearrange("p d c -> p (d c)")
                W = TPG * P
                for g in range(PAIR):
                    for c in range(2):
                        last = A.activation(h_t[:, h, c, g * W:(g + 1) * W],
                                            p_turn[:, c * T * P + g * W:c * T * P + (g + 1) * W], ACT.Relu,
                                            bias=gb1[:, bass.ds(d[g] * 4 + 2 + c, 1)],
                                            scale=gb1[:, bass.ds(d[g] * 4 + c, 1)])
                last.then_inc(ht_ready, 1)

            pipeline(act, STEPS, AHEAD, [(3, deviation1), (5, relu1), (1, copy_ea), (7, deviation2)])

        @block.vector
        def _(dve):
            engine = Waits(dve, woken["dve"])
            V = nc.vector
            V.memset(acc[:, :, :], 0.0).then_inc(cleared, 1)
            V.memset(ea1[:, :, :, EA:EA + 1], 1.0).then_inc(cleared, 1)
            dve.wait_ge(cleared, 2)
            rows = w["rows"]

            def row(base, d):
                return rows[:, :, :].rearrange("p i f -> p (i f)")[:, bass.ds(d * D + base * D, D)].unsqueeze(1)\
                    .to_broadcast([P, TPG, D])

            def take(s):
                r = s.slot(RING)
                engine.wait_ge(rec_in[r], s.turn(RING, 16, 16))
                V.tensor_copy(index[:, r, :], rec[:, r, :, R_COL]).then_inc(index_ready, 1)
                V.tensor_tensor(ea1[:, r, :, 0:EA], rec[:, r, :, 0:EA],
                                rec[:, r, :, R_ATT:R_ATT + 1].to_broadcast([P, T, EA]), ALU.mult)\
                    .then_inc(ea1_ready, 1)

            def join(s):
                r, h = s.slot(RING), s.slot(2)
                engine.wait_ge(u_in[r], s.turn(RING, 16 * T, 16 * T))
                engine.wait_ge(v_in_psum, s.n(1, 1))
                for j in range(T):
                    last = V.scalar_tensor_tensor(out=v[:, r, j, :], in0=u[:, r, j, :],
                                                  scalar=rec[:, r, j, R_ATT:R_ATT + 1],
                                                  in1=p_v[:, j * H:(j + 1) * H], op0=ALU.mult, op1=ALU.add)
                last.then_inc(v_ready, 1)

            def invert1(s):
                h = s.slot(2)
                engine.wait_ge(dev1_ready, s.n(1, 1))
                V.reciprocal(inv[:, h, 0, :], dev[:, h, 0, :]).then_inc(inv1_done, 1)

            def invert2(s):
                h = s.slot(2)
                engine.wait_ge(dev2_ready, s.n(1, 1))
                V.reciprocal(inv[:, h, 1, :], dev[:, h, 1, :]).then_inc(norm2, 1)

            def norm1(s):
                h = s.slot(2)
                engine.wait_ge(inv1_done, s.n(1, 1))
                for j in range(T):
                    last = V.tensor_scalar(vn[:, s.slot(RING), j, :], v[:, s.slot(RING), j, :], inv[:, h, 0, j:j + 1], None, ALU.mult)
                last.then_inc(vn_ready, 1)

            def bias2(s):
                h = s.slot(2)
                d = [group_value(dve, 1, s, g, 1) for g in range(PAIR)]
                engine.wait_ge(v2_in_psum, s.n(1, 1))
                for g in range(PAIR):
                    tiles = slice(g * TPG, (g + 1) * TPG)
                    last = V.tensor_tensor(v2[:, h, tiles, :],
                                           p_v2[:, :].rearrange("p (t f) -> p t f", t=T)[:, tiles, :],
                                           row(B2, d[g]), ALU.add)
                last.then_inc(v2_ready, 1)

            def norm2_bias(s):
                h = s.slot(2)
                d = [group_value(dve, 1, s, g, 1) for g in range(PAIR)]
                engine.wait_ge(norm2, s.n(3, 1))
                for j in range(T):
                    g2 = rows[:, :, :].rearrange("p i f -> p (i f)")[:, bass.ds(d[j // TPG] * D + G2 * D, D)]
                    last = V.scalar_tensor_tensor(out=h2[:, h, j, :], in0=v2[:, h, j, :],
                                                  scalar=inv[:, h, 1, j:j + 1], in1=g2, op0=ALU.mult, op1=ALU.mult)
                last.then_inc(norm2, 1)
                engine.wait_ge(norm2, s.n(3, 2))
                for g in range(PAIR):
                    tiles = slice(g * TPG, (g + 1) * TPG)
                    last = V.tensor_tensor(h2[:, h, tiles, :], h2[:, h, tiles, :], row(BE2, d[g]), ALU.add)
                last.then_inc(norm2, 1)

            def relu2(s):
                h = s.slot(2)
                engine.wait_ge(norm2, s.n(3, 3))
                V.tensor_scalar(h2[:, h, :, :], h2[:, h, :, :], 0.0, None, ALU.max).then_inc(h2_ready, 1)

            def add(s):
                b = [group_value(dve, 0, s, g, BINS - 1) for g in range(PAIR)]
                engine.wait_ge(summed, s.n(1, 1))
                for g in range(PAIR):
                    if g or s.trip is not None or s.at >= 1:
                        engine.wait_ge(added, s.n(PAIR, g))
                    into = acc[:, bass.ds(b[g], 1), :]
                    V.tensor_tensor(into, into, p_sum[:, g * D:(g + 1) * D].unsqueeze(1), ALU.add).then_inc(added, 1)

            pipeline(dve, STEPS, AHEAD, [(4, invert1), (8, invert2), (7, bias2), (4, norm1), (0, take), (8, norm2_bias),
                                          (9, add), (2, join), (8, relu2)])


def phase_first_nodes(kit, w, acc):
    nc, t, out, dram, woken, x_s, ident, iota_f, eps_s, zero_s, tab_s = kit
    with ExitStack() as ctx:
        def sb(name, shape, dt=F32):
            return ctx.enter_context(nc.sbuf_tensor("n_" + name, shape, dt))

        def ps(name):
            return ctx.enter_context(nc.psum_tensor("n_" + name, [P, 512], F32))

        def sem(name):
            return ctx.enter_context(nc.semaphore(name))

        flow = sb("flow", [P, RING, 2, D])
        xb = sb("xb", [P, RING, DX])
        turned = sb("turned", [P, RING, 3, P])
        pre = sb("pre", [P, RING, 2, D])
        act_ = sb("normed", [P, RING, 2, D])
        y = sb("y", [P, RING, DX])
        x1 = sb("x1", [P, RING, DX])
        junk = sb("junk", [P, RING, 2, D])
        sq, dev, inv = sb("sq", [P, RING, 2]), sb("dev", [P, RING, 2]), sb("inv", [P, RING, 2])
        bn, mv = sb("bn", [P, RING, 6]), sb("mv", [P, RING, 2])
        dev3, inv3 = sb("dev3", [P, RING, 1]), sb("inv3", [P, RING, 1])
        p_turn = [ps(f"p_turn{i}") for i in range(2)]
        p_pre = [ps(f"p_pre{i}") for i in range(2)]
        staged, turn_done, turned_ready = sem("n_staged"), sem("n_turn_done"), sem("n_turned_ready")
        product_done, pre_ready, squared, dev_ready = sem("n_product"), sem("n_pre"), sem("n_squared"), sem("n_dev")
        chain, mv_ready, dev3_ready = sem("n_chain"), sem("n_mv"), sem("n_dev3")
        chain3, x1_ready, kept = sem("n_chain3"), sem("n_x1_ready"), sem("n_kept")
        stored = [sem(f"n_stored{i}") for i in range(RING)]
        block = ctx.enter_context(nc.Block())
        C = 7

        @block.gpsimd
        def _(pool):
            engine = Waits(pool, woken["pool"])

            def stage(s):
                r = s.slot(RING)
                if s.trip is not None or s.at >= RING:
                    engine.wait_ge(mv_ready, s.n(1, 1 - RING))
                for i, base in enumerate((NBLK, 0)):
                    nc.gpsimd.tensor_copy(flow[:, r, i, :].unsqueeze(1), acc[:, bass.ds(s.n(1, base), 1), :])
                nc.gpsimd.tensor_copy(xb[:, r, :].unsqueeze(1), x_s[:, bass.ds(s.n(), 1), :]).then_inc(staged, 1)

            def keep(s):
                r = s.slot(RING)
                engine.wait_ge(x1_ready, s.n(1, 1))
                nc.gpsimd.tensor_copy(x_s[:, bass.ds(s.n(), 1), :], x1[:, r, :].unsqueeze(1)).then_inc(kept, 1)

            pipeline(pool, NBLK, RING, [(3, keep), (0, stage)])

        @block.tensor
        def _(pe):
            engine = Waits(pe, woken["pe"])

            def turn(s):
                r, h = s.slot(RING), s.slot(2)
                engine.wait_ge(staged, s.n(1, 1))
                for i, src in enumerate((flow[:, r, 0, :], flow[:, r, 1, :], xb[:, r, 0:D])):
                    last = nc.tensor.transpose(p_turn[h][:, i * P:(i + 1) * P], src, ident[:, :])
                last.then_inc(turn_done, 1)

            def product(s):
                r, h = s.slot(RING), s.slot(2)
                engine.wait_ge(turned_ready, s.n(1, 1))
                if s.trip is not None or s.at >= 2:
                    engine.wait_ge(pre_ready, s.n(1, -1))
                for i in range(2):
                    nc.tensor.matmul(p_pre[h][:, 0:D], turned[:, r, i, :], w["nsw"][:, i, :], start=(i == 0),
                                     stop=(i == 1))
                nc.tensor.matmul(p_pre[h][:, D:2 * D], turned[:, r, 2, :], w["nsw"][:, 2, :], start=True, stop=True)\
                    .then_inc(product_done, 1)

            pipeline(pe, NBLK, RING, [(1, product), (0, turn)])

        @block.scalar
        def _(act):
            engine = Waits(act, woken["act"])
            A = nc.scalar

            def copy(s):
                r, h = s.slot(RING), s.slot(2)
                engine.wait_ge(turn_done, s.n(1, 1))
                A.copy(turned[:, r, :, :].rearrange("p i f -> p (i f)"), p_turn[h][:, 0:3 * P])\
                    .then_inc(turned_ready, 1)

            def deviation(s):
                r = s.slot(RING)
                engine.wait_ge(pre_ready, s.n(1, 1))
                for i in range(2):
                    A.activation(junk[:, r, i, :], pre[:, r, i, :], ACT.Square, bias=zero_s[:, 0:1],
                                 accum_out=sq[:, r, i:i + 1]).then_inc(squared, 1)
                engine.wait_ge(squared, s.n(2, 2))
                A.activation(dev[:, r, :], sq[:, r, :], ACT.Sqrt, bias=eps_s[:, 0:1], scale=1.0 / D)\
                    .then_inc(dev_ready, 1)

            def deviation3(s):
                r = s.slot(RING)
                engine.wait_ge(mv_ready, s.n(1, 1))
                A.activation(dev3[:, r, :], mv[:, r, 1:2], ACT.Sqrt, bias=eps_s[:, 0:1]).then_inc(dev3_ready, 1)

            pipeline(act, NBLK, RING, [(2, deviation3), (1, deviation), (0, copy)])

        @block.vector
        def _(dve):
            engine = Waits(dve, woken["dve"])
            V = nc.vector
            rows = w["rows"]

            def biased(s):
                r, h = s.slot(RING), s.slot(2)
                engine.wait_ge(product_done, s.n(1, 1))
                V.tensor_tensor(pre[:, r, :, :], p_pre[h][:, 0:2 * D].rearrange("p (i f) -> p i f", i=2),
                                rows[:, NSB:NSB + 2, :], ALU.add).then_inc(pre_ready, 1)

            def mix(s):
                r = s.slot(RING)
                links = [0]

                def link(ins):
                    links[0] += 1
                    ins.then_inc(chain, 1)
                    engine.wait_ge(chain, s.n(C, links[0]))

                engine.wait_ge(dev_ready, s.n(1, 1))
                link(V.reciprocal(inv[:, r, :], dev[:, r, :]))
                for i in range(2):
                    last = V.scalar_tensor_tensor(out=act_[:, r, i, :], in0=pre[:, r, i, :], scalar=inv[:, r, i:i + 1],
                                                  in1=rows[:, NSG + i, :], op0=ALU.mult, op1=ALU.mult)
                link(last)
                link(V.tensor_tensor(pre[:, r, :, :], act_[:, r, :, :], rows[:, NSBE:NSBE + 2, :], ALU.add))
                link(V.tensor_scalar(act_[:, r, :, :], pre[:, r, :, :], 0.0, None, ALU.max))
                link(V.tensor_tensor(act_[:, r, 0, :], act_[:, r, 0, :], act_[:, r, 1, :], ALU.add))
                V.tensor_tensor(y[:, r, 0:D], act_[:, r, 0, :], xb[:, r, 0:D], ALU.add)
                link(V.tensor_scalar(y[:, r, D:DX], xb[:, r, D:DX], 2.0, None, ALU.mult))
                link(V.bn_stats(bn[:, r, :], y[:, r, :]))
                V.bn_aggr(mv[:, r, :], bn[:, r, :]).then_inc(mv_ready, 1)

            def norm3(s):
                r = s.slot(RING)
                engine.wait_ge(dev3_ready, s.n(1, 1))
                engine.wait_ge(stored[r], s.turn(RING, 32))
                if s.trip is not None or s.at >= RING:
                    engine.wait_ge(kept, s.n(1, 1 - RING))
                V.reciprocal(inv3[:, r, :], dev3[:, r, :]).then_inc(chain3, 1)
                engine.wait_ge(chain3, s.n(1, 1))
                V.tensor_scalar(x1[:, r, :], y[:, r, :], mv[:, r, 0:1], inv3[:, r, :], ALU.subtract, ALU.mult)\
                    .then_inc(x1_ready, 1)

            pipeline(dve, NBLK, RING, [(3, norm3), (2, mix), (1, biased)])

        @block.sync
        def _(sp):
            engine = Waits(sp, woken["sp"])

            def store(s):
                r = s.slot(RING)
                engine.wait_ge(x1_ready, s.n(1, 1))
                for d in range(2):
                    sp.dma_start(dram["x1"][bass.ds(s.n(P, d * NPAD), P), :], x1[:, r, :]).then_inc(stored[r], 16)

            pipeline(sp, NBLK, RING, [(0, store)])
            for r in range(RING):
                engine.wait_ge(stored[r], 32 * len(range(r, NBLK, RING)))


def phase_second_edges(kit, acc, rec_in, x_in):
    nc, t, out, dram, woken, x_s, ident, iota_f, eps_s, zero_s, tab_s = kit
    T = TPG
    BANK = 512
    with ExitStack() as ctx:
        def sb(name, shape, dt=F32):
            return ctx.enter_context(nc.sbuf_tensor("m_" + name, shape, dt))

        def ps(name):
            return ctx.enter_context(nc.psum_tensor("m_" + name, [P, BANK], F32))

        def sem(name):
            return ctx.enter_context(nc.semaphore(name))

        rec = sb("rec", [P, AHEAD, T, RW])
        index = sb("index", [P, AHEAD, T], I32)
        q = sb("q", [P, AHEAD, T, QW])
        prod = sb("prod", [P, RING, T, 3 * M1])
        onehot = sb("onehot", [P, RING, T, P])
        p_lo = [ps(f"p_lo{i}") for i in range(2)]
        p_hi = [ps(f"p_hi{i}") for i in range(2)]
        loads = [GROUPS // PAIR // RING * 16 if i < RING else 0 for i in range(AHEAD)]
        gathers = [loads_of * PAIR * T for loads_of in loads]
        rec_used, index_ready, cleared = sem("m_rec_used"), sem("m_index_ready"), sem("m_cleared")
        prod_done, q_ready, summed, added = sem("m_prod_done"), sem("m_q_ready"), sem("m_summed"), sem("m_added")
        scaled = sem("m_scaled")
        block = ctx.enter_context(nc.Block())

        @block.sync
        def _(sp):
            engine = Waits(sp, woken["sp"])

            def load(s):
                r = s.slot(AHEAD)
                engine.wait_ge(rec_used, s.n(1, 1 - AHEAD))
                if s.trip is not None or s.at >= AHEAD:
                    engine.wait_ge(scaled, s.n(1, 1 - AHEAD))
                sp.dma_start(rec[:, r, :, :].rearrange("p t w -> p (t w)"),
                             dram["rec"].rearrange("(g p t) w -> g p (t w)", p=P, t=T)[bass.ds(s.n(), 1), :, :]
                             .rearrange("g p w -> (g p) w")).then_inc(rec_in[r], 16)

            pipeline(sp, GROUPS, AHEAD, [(0, load)])

        @block.gpsimd
        def _(pool):
            engine = Waits(pool, woken["pool"])

            def gather(s):
                r = s.slot(AHEAD)
                engine.wait_ge(index_ready, s.n(1, 1))
                for j in range(T):
                    nc.gpsimd.indirect_dma_start(
                        q[:, r, j, 0:DX], None, dram["x1"],
                        bass.IndirectOffsetOnAxis(ap=index[:, r, j:j + 1], axis=0)).then_inc(x_in[r], 16)

            pipeline(pool, GROUPS, AHEAD, [(0, gather)])

        @block.scalar
        def _(act):
            engine = Waits(act, woken["act"])

            def scale(s):
                r = s.slot(AHEAD)
                engine.wait_ge(x_in[r], s.turn(AHEAD, 16 * T, 16 * T + gathers[r]))
                for j in range(T):
                    last = nc.scalar.mul(q[:, r, j, Q_E0:Q_E0 + DX], q[:, r, j, 0:DX], rec[:, r, j, R_E0:R_E0 + 1])
                last.then_inc(scaled, 1)

            pipeline(act, GROUPS, AHEAD, [(3, scale)])

        @block.tensor
        def _(pe):
            engine = Waits(pe, woken["pe"])

            def node_sum(s):
                r, h = s.slot(AHEAD), s.slot(2)
                engine.wait_ge(q_ready, s.n(1, 1))
                engine.wait_ge(scaled, s.n(1, 1))
                if s.trip is not None or s.at >= 2:
                    engine.wait_ge(added, s.n(1, -1))
                for p, lo, hi in ((p_lo[h], 0, BANK), (p_hi[h], BANK, QW)):
                    for j in range(T):
                        last = nc.tensor.matmul(p[:, 0:hi - lo], onehot[:, s.slot(RING), j, :], q[:, r, j, lo:hi],
                                                start=(j == 0), stop=(j == T - 1))
                last.then_inc(summed, 1)

            pipeline(pe, GROUPS, AHEAD, [(4, node_sum)])

        @block.vector
        def _(dve):
            engine = Waits(dve, woken["dve"])
            V = nc.vector
            V.memset(acc[:, :, :], 0.0).then_inc(cleared, 1)
            dve.wait_ge(cleared, 1)

            def take(s):
                r = s.slot(AHEAD)
                engine.wait_ge(rec_in[r], s.turn(AHEAD, 16, 16 + loads[r]))
                V.tensor_copy(index[:, r, :], rec[:, r, :, R_COL]).then_inc(index_ready, 1)

            def spread(s):
                r = s.slot(AHEAD)
                engine.wait_ge(x_in[r], s.turn(AHEAD, 16 * T, 16 * T + gathers[r]))
                e1 = rec[:, r, :, R_E1:R_E1 + 3]
                V.tensor_tensor(prod[:, s.slot(RING), :, :].rearrange("p t (u k) -> p t u k", k=3),
                                q[:, r, :, M0:DX].rearrange("p t (u k) -> p t u k", k=3),
                                e1.unsqueeze(2).to_broadcast([P, T, M1, 3]), ALU.mult).then_inc(prod_done, 1)
                for j in range(T):
                    V.tensor_scalar(onehot[:, s.slot(RING), j, :], iota_f[:, :], rec[:, r, j, R_LOC1:R_LOC1 + 1], None,
                                    ALU.is_equal)
                last = V.tensor_tensor(q[:, r, :, Q_E1:Q_Z].rearrange("p t (k u) -> p t k u", k=3),
                                       q[:, r, :, 0:M0].unsqueeze(2).to_broadcast([P, T, 3, M0]),
                                       e1.unsqueeze(3).to_broadcast([P, T, 3, M0]), ALU.mult)
                last.then_inc(rec_used, 1)
                engine.wait_ge(prod_done, s.n(1, 1))
                V.reduce_sum(q[:, r, :, Q_Z:QW], prod[:, s.slot(RING), :, :].rearrange("p t (u k) -> p t u k", k=3),
                             axis=AX_X).then_inc(q_ready, 1)

            def add(s):
                h = s.slot(2)
                b = dve.value_load(tab_s[0:1, 2, bass.ds(s.n(), 1)], min_val=0, max_val=NBLK - 1)
                engine.wait_ge(summed, s.n(1, 1))
                if s.trip is not None or s.at >= 1:
                    engine.wait_ge(added, s.n())
                for p, lo, hi in ((p_lo[h], 0, BANK), (p_hi[h], BANK, QW)):
                    into = acc[:, bass.ds(b, 1), lo:hi]
                    last = V.tensor_tensor(into, into, p[:, 0:hi - lo].unsqueeze(1), ALU.add)
                last.then_inc(added, 1)

            pipeline(dve, GROUPS, AHEAD, [(5, add), (0, take), (3, spread)])


def phase_second_nodes(kit, acc):
    nc, t, out, dram, woken, x_s, ident, iota_f, eps_s, zero_s, tab_s = kit
    F0, F1 = M0 * M0 + M1 * M1, 2 * M0 * M1
    c_msg = (M0 + M1) ** -0.5
    c0, c1 = F0 ** -0.5, F1 ** -0.5
    inv3_ = 3.0 ** -0.5
    QC = -(-QW // P)
    with ExitStack() as ctx:
        def sb(name, shape, dt=F32):
            return ctx.enter_context(nc.sbuf_tensor("f_" + name, shape, dt))

        def ps(name):
            return ctx.enter_context(nc.psum_tensor("f_" + name, [P, 512], F32))

        def sem(name):
            return ctx.enter_context(nc.semaphore(name))

        mix_w = sb("mix_w", [P, QC, DX])
        lin_w = sb("lin_w", [P, 2, DX])
        w000 = sb("w000", [M0, M0 * M0])
        w011 = sb("w011", [M0, M1 * M1])
        w101 = sb("w101", [M0, M1 * M1])
        w110 = sb("w110", [P, M1 * M1 // P, M0])
        xb = sb("xb", [P, 2, DX])
        gb = sb("gb", [P, 1, QW])
        x_t = sb("x_t", [P, 1, 2, P])
        g_t = sb("g_t", [P, 1, QC, P])
        agg = sb("agg", [P, 2, DX])
        a_t = sb("a_t", [M0, 1, P])
        outer = sb("outer", [P, M1 * M1])
        outer2 = sb("outer2", [P, M1 * M1])
        o_t = sb("o_t", [P, M1 * M1 // P, P])
        m0 = sb("m0", [P, M0 // 2, M0])
        m1 = m0[:, :, :].rearrange("p v w -> p (v w)").rearrange("p (v w) -> p v w", w=M1)
        red0 = sb("red0", [P, 2, M0])
        red = sb("red", [P, 2, DX])
        y = sb("y", [P, 2, DX])
        fin = sb("fin", [P, 2, DX])
        bn, mv, dev, inv = sb("bn", [P, 2, 6]), sb("mv", [P, 2, 2]), sb("dev", [P, 2, 1]), sb("inv", [P, 2, 1])
        raw = sb("raw", [M0, 7, M0])
        p_x = ps("p_x")
        p_g = ps("p_g")
        p_m = ps("p_m")
        p_b = [ps(f"p_b{i}") for i in range(5)]

        loaded, zeroed, laid, mixed = sem("w_loaded"), sem("w_zeroed"), sem("w_laid"), sem("w_mixed")
        chain0 = sem("w_chain")
        staged, g_turned, xt_ready = sem("f_staged"), sem("f_g_turned"), sem("f_xt_ready")
        gt_ready, agg_done, agg_ready = sem("f_gt_ready"), sem("f_agg_done"), sem("f_agg_ready")
        a_turned, at_ready = sem("f_a_turned"), sem("f_at_ready")
        bank_full, bank_free = sem("f_bank_full"), sem("f_bank_free")
        outer_step, outer_ready = sem("f_outer_step"), sem("f_outer_ready")
        o_turned, ot_ready, linear_done = sem("f_o_turned"), sem("f_ot_ready"), sem("f_linear_done")
        chain, mv_ready, dev_ready = sem("f_chain"), sem("f_mv_ready"), sem("f_dev_ready")
        inv_done, fin_ready = sem("f_inv_done"), sem("f_fin_ready")
        stored = [sem(f"f_stored{i}") for i in range(2)]
        o_half = sem("f_o_half")

        L = "L1_gnn_"
        small = [("lm0", M0, M0, M0 ** -0.5), ("lm1", M1, M1, M1 ** -0.5), ("wm000", M0, M0, c_msg),
                 ("wm101", M1, M1, c_msg), ("wm011", M0, M1, c_msg), ("wm110", M1, M0, c_msg * inv3_),
                 ("lu0", M0, M0, M0 ** -0.5), ]
        small2 = [("lu1", M1, M1, M1 ** -0.5)]
        raw2 = sb("raw2", [M1, M1])

        with nc.Block() as block:
            mix = dram["mix"]

            def vec(base, k, rows, first_col):
                return mix[base:base + 3 * rows, :].rearrange("(u k) c -> k u c", k=3)[k, :, first_col:DX]\
                    .rearrange("u (w k) -> k u w", k=3)[k]

            @block.vector
            def _(dve):
                n = [0]

                def link(ins):
                    n[0] += 1
                    ins.then_inc(chain0, 1)
                    dve.wait_ge(chain0, n[0])

                nc.vector.memset(g_t[:, :, :, :], 0.0).then_inc(zeroed, 1)
                nc.vector.memset(mix_w[:, :, :], 0.0).then_inc(zeroed, 1)
                nc.vector.memset(lin_w[:, :, :], 0.0).then_inc(zeroed, 1)
                dve.wait_ge(loaded, 16 * 13)
                for i, (name, k, m, scale) in enumerate(small):
                    nc.vector.tensor_scalar(raw[0:k, i, 0:m], raw[0:k, i, 0:m], scale, None, ALU.mult)\
                        .then_inc(mixed, 1)
                nc.vector.tensor_scalar(raw2[:, :], raw2[:, :], M1 ** -0.5, None, ALU.mult).then_inc(mixed, 1)
                nc.vector.tensor_scalar(w000[:, :], w000[:, :], c0, None, ALU.mult)
                nc.vector.tensor_scalar(w011[:, :], w011[:, :], c1, None, ALU.mult)
                nc.vector.tensor_scalar(w101[:, :], w101[:, :], c1, None, ALU.mult)
                nc.vector.tensor_scalar(w110[:, :, :], w110[:, :, :], c0 * inv3_, None, ALU.mult)

            @block.sync
            def _(sp):
                for i, (name, k, m, scale) in enumerate(small):
                    src = t[L + name]
                    if len(src.shape) == 3:
                        src = src.rearrange("u o w -> u (o w)")
                    sp.dma_start(raw[0:k, i, 0:m], src).then_inc(loaded, 16)
                sp.dma_start(raw2[:, :], t[L + "lu1"]).then_inc(loaded, 16)
                sp.dma_start(w000[:, :], t[L + "wu000"].rearrange("u v w -> u (v w)")).then_inc(loaded, 16)
                sp.dma_start(w011[:, :], t[L + "wu011"].rearrange("u v w -> u (v w)")).then_inc(loaded, 16)
                sp.dma_start(w101[:, :].rearrange("v (u w) -> v u w", u=M1),
                             t[L + "wu101"].rearrange("u v w -> v u w")).then_inc(loaded, 16)
                sp.dma_start(w110[:, :, :], t[L + "wu110"].rearrange("u v w -> (u v) w")
                             .rearrange("(c k) w -> k c w", k=P)).then_inc(loaded, 16)
                sp.dma_start(red[:, 0, :], t["x"][0:P, :]).then_inc(loaded, 16)
                sp.wait_ge(zeroed, 2)
                zeros = mix_w[:, :, :].rearrange("p c f -> p (c f)")
                rows = 88
                for half in range(2):
                    sp.dma_start(mix.rearrange("(h p r) c -> h p (r c)", h=2, p=rows)[half],
                                 zeros[0:rows, 0:(QW + DX) // (2 * rows) * DX]).then_inc(laid, 16)
                sp.wait_ge(laid, 32)
                sp.wait_ge(mixed, 8)
                placed = [(mix[0:M0, 0:M0], raw[:, 0, :]), (mix[Q_E0:Q_E0 + M0, 0:M0], raw[:, 2, :]),
                          (mix[Q_Z:QW, 0:M0], raw[0:M1, 5, :]), (mix[QW:QW + M0, 0:M0], raw[:, 6, :])]
                for k in range(3):
                    placed += [(vec(M0, k, M1, M0), raw[0:M1, 1, 0:M1]),
                               (vec(Q_E0 + M0, k, M1, M0), raw[0:M1, 3, 0:M1]),
                               (mix[Q_E1 + k * M0:Q_E1 + (k + 1) * M0, M0:DX].rearrange("u (w k) -> k u w", k=3)[k],
                                raw[:, 4, 0:M1]),
                               (vec(QW + M0, k, M1, M0), raw2[:, :])]
                for dst, src in placed:
                    sp.dma_start(dst, src).then_inc(laid, 16)
                sp.wait_ge(laid, 16 * (2 + len(placed)))
                n = 2 + len(placed)
                for dst, base, rows in ((mix_w, 0, QW), (lin_w, QW, DX)):
                    for c in range(-(-rows // P)):
                        k = min(P, rows - c * P)
                        sp.dma_start(dst[0:k, c, :], mix[base + c * P:base + c * P + k, :]).then_inc(laid, 16)
                        n += 1
                sp.wait_ge(laid, 16 * n)

        BANKS = 12
        NPB = len(p_b)
        CH = 10
        with nc.Block() as block:
            @block.gpsimd
            def _(pool):
                engine = Waits(pool, woken["pool"])
                G = nc.gpsimd

                def stage(s):
                    h = s.slot(2)
                    if s.trip is not None or s.at >= 2:
                        engine.wait_ge(mv_ready, s.n(1, -1))
                        engine.wait_ge(gt_ready, s.n())
                    G.tensor_copy(xb[:, h, :].unsqueeze(1), x_s[:, bass.ds(s.n(), 1), :])
                    G.tensor_copy(gb[:, 0, :].unsqueeze(1), acc[:, bass.ds(s.n(), 1), :]).then_inc(staged, 1)

                def outer_product(s):
                    h = s.slot(2)
                    engine.wait_ge(agg_ready, s.n(1, 1))
                    if s.trip is not None or s.at >= 1:
                        engine.wait_ge(o_turned, s.n())
                    x1 = xb[:, h, M0:DX].rearrange("p (u k) -> p u k", k=3)
                    a1 = agg[:, h, M0:DX].rearrange("p (v k) -> p v k", k=3)

                    def term(dst, k):
                        return G.tensor_tensor(dst.rearrange("p (u v) -> p u v", u=M1),
                                               x1[:, :, k:k + 1].to_broadcast([P, M1, M1]),
                                               a1[:, :, k].unsqueeze(1).to_broadcast([P, M1, M1]), ALU.mult)

                    term(outer[:, :], 0)
                    term(outer2[:, :], 1).then_inc(outer_step, 1)
                    engine.wait_ge(outer_step, s.n(3, 1))
                    G.tensor_tensor(outer[:, :], outer[:, :], outer2[:, :], ALU.add).then_inc(outer_step, 1)
                    engine.wait_ge(outer_step, s.n(3, 2))
                    term(outer2[:, :], 2).then_inc(outer_step, 1)
                    engine.wait_ge(outer_step, s.n(3, 3))
                    G.tensor_tensor(outer[:, :], outer[:, :], outer2[:, :], ALU.add).then_inc(outer_ready, 1)

                pipeline(pool, NBLK, 2, [(1, outer_product), (0, stage)])

            @block.tensor
            def _(pe):
                engine = Waits(pe, woken["pe"])
                M = nc.tensor.matmul

                def turn(s):
                    h = s.slot(2)
                    engine.wait_ge(staged, s.n(1, 1))
                    nc.tensor.transpose(p_x[:, 0:P], xb[:, h, 0:P], ident[:, :])
                    nc.tensor.transpose(p_x[0:DX - P, P:2 * P], xb[:, h, P:DX], ident[:, :])
                    for c in range(QC):
                        k = min(P, QW - c * P)
                        p, at = (p_g, c * P) if c < 4 else (p_x, 2 * P)
                        last = nc.tensor.transpose(p[0:k, at:at + P], gb[:, 0, c * P:c * P + k], ident[:, :])
                    last.then_inc(g_turned, 1)

                def aggregate(s):
                    h = s.slot(2)
                    engine.wait_ge(gt_ready, s.n(1, 1))
                    for c in range(QC):
                        last = M(p_g[:, 0:DX], g_t[:, 0, c, :], mix_w[:, c, :], start=(c == 0), stop=(c == QC - 1))
                    last.then_inc(agg_done, 1)

                def turn_a(s):
                    h = s.slot(2)
                    engine.wait_ge(agg_ready, s.n(1, 1))
                    nc.tensor.transpose(p_x[0:M0, 3 * P:4 * P], agg[:, h, 0:M0], ident[:, :]).then_inc(a_turned, 1)

                def bank(s, i, lhs, rhs, n):
                    b = p_b[i % NPB]
                    M(b[:, 0:n], lhs, rhs, start=True, stop=True).then_inc(bank_full, 1)

                def banks(s):
                    h = s.slot(2)
                    engine.wait_ge(xt_ready, s.n(1, 1))
                    for i in range(BANKS):
                        if i >= NPB or s.trip is not None or s.at >= 1:
                            held = i - NPB if i >= NPB else max(range(i, BANKS, NPB)) - BANKS
                            engine.wait_ge(bank_free, s.n(BANKS, held + 1))
                        if i < 8:
                            bank(s, i, x_t[0:M0, 0, 0, :], w000[:, i * 512:(i + 1) * 512], 512)
                        elif i < 10:
                            bank(s, i, x_t[0:M0, 0, 0, :], w011[:, (i - 8) * 512:(i - 7) * 512], 512)
                        else:
                            if i == 10:
                                engine.wait_ge(at_ready, s.n(1, 1))
                            bank(s, i, a_t[:, 0, :], w101[:, (i - 10) * 512:(i - 9) * 512], 512)

                def turn_outer(s):
                    engine.wait_ge(outer_ready, s.n(1, 1))
                    for i in range(8):
                        b = p_g if i < 4 else p_x
                        last = nc.tensor.transpose(b[:, (i % 4) * P:(i % 4 + 1) * P], outer[:, i * P:(i + 1) * P],
                                                   ident[:, :])
                        if i % 4 == 3:
                            last.then_inc(o_turned if i == 7 else o_half, 1)

                def linear(s):
                    h = s.slot(2)
                    engine.wait_ge(ot_ready, s.n(2, 2))
                    if s.trip is not None or s.at >= 1:
                        engine.wait_ge(chain, s.n(CH, 8 - CH))
                    M(p_m[:, 0:DX], x_t[:, 0, 0, :], lin_w[:, 0, :], start=True, stop=False, skip_group_check=True)
                    M(p_m[:, 0:DX], x_t[0:DX - P, 0, 1, :], lin_w[0:DX - P, 1, :], start=False, stop=False,
                      skip_group_check=True)
                    for i in range(8):
                        last = M(p_m[:, 0:M0], o_t[:, i, :], w110[:, i, :], start=False, stop=(i == 7),
                                 skip_group_check=True)
                    last.then_inc(linear_done, 1)

                def all_of(s):
                    if s.trip is not None or s.at >= 1:
                        engine.wait_ge(ot_ready, s.n(2))
                    turn(s)
                    aggregate(s)
                    turn_a(s)
                    banks(s)
                    turn_outer(s)
                    linear(s)

                pipeline(pe, NBLK, 2, [(0, all_of)])

            @block.scalar
            def _(act):
                engine = Waits(act, woken["act"])
                A = nc.scalar

                def copies(s):
                    h = s.slot(2)
                    engine.wait_ge(g_turned, s.n(1, 1))
                    A.copy(x_t[:, 0, 0, :], p_x[:, 0:P])
                    A.copy(x_t[0:DX - P, 0, 1, :], p_x[0:DX - P, P:2 * P]).then_inc(xt_ready, 1)
                    A.copy(g_t[:, 0, 0:4, :].rearrange("p c n -> p (c n)"), p_g[:, :])
                    A.copy(g_t[0:QW - 4 * P, 0, 4, :], p_x[0:QW - 4 * P, 2 * P:3 * P]).then_inc(gt_ready, 1)
                    engine.wait_ge(agg_done, s.n(1, 1))
                    A.copy(agg[:, h, :], p_g[:, 0:DX]).then_inc(agg_ready, 1)
                    engine.wait_ge(a_turned, s.n(1, 1))
                    A.copy(a_t[:, 0, :], p_x[0:M0, 3 * P:4 * P]).then_inc(at_ready, 1)

                def copies2(s):
                    engine.wait_ge(o_half, s.n(1, 1))
                    A.copy(o_t[:, 0:4, :].rearrange("p c n -> p (c n)"), p_g[:, :]).then_inc(ot_ready, 1)
                    engine.wait_ge(o_turned, s.n(1, 1))
                    A.copy(o_t[:, 4:8, :].rearrange("p c n -> p (c n)"), p_x[:, :]).then_inc(ot_ready, 1)

                def deviation(s):
                    h = s.slot(2)
                    engine.wait_ge(mv_ready, s.n(1, 1))
                    A.activation(dev[:, h, :], mv[:, h, 1:2], ACT.Sqrt, bias=eps_s[:, 0:1]).then_inc(dev_ready, 1)

                pipeline(act, NBLK, 2, [(0, copies), (1, deviation), (0, copies2)])

            @block.vector
            def _(dve):
                engine = Waits(dve, woken["dve"])
                V = nc.vector

                def main(s):
                    h = s.slot(2)
                    links = [0]

                    def link(ins):
                        links[0] += 1
                        ins.then_inc(chain, 1)
                        engine.wait_ge(chain, s.n(CH, links[0]))

                    engine.wait_ge(agg_ready, s.n(1, 1))
                    for half in range(2):
                        for i in range(4 * half, 4 * half + 4):
                            engine.wait_ge(bank_full, s.n(BANKS, i + 1))
                            V.tensor_tensor(m0[:, (i % 4) * 8:(i % 4 + 1) * 8, :],
                                            p_b[i % NPB][:, :].rearrange("p (v w) -> p v w", w=M0),
                                            agg[:, h, i * 8:(i + 1) * 8].unsqueeze(2).to_broadcast([P, 8, M0]),
                                            ALU.mult).then_inc(bank_free, 1)
                        engine.wait_ge(bank_free, s.n(BANKS, 4 * half + 4))
                        link(V.reduce_sum(red0[:, half, :], m0[:, :, :].rearrange("p v w -> p w v"), axis=AX_X))
                    V.tensor_tensor(red[:, h, 0:M0], red0[:, 0, :], red0[:, 1, :], ALU.add)
                    a1 = agg[:, h, M0:DX].rearrange("p (v k) -> p v k", k=3)
                    x1 = xb[:, h, M0:DX].rearrange("p (u k) -> p u k", k=3)
                    engine.wait_ge(bank_full, s.n(BANKS, 12))
                    for k in range(3):
                        for i in range(4):
                            c = (a1 if i < 2 else x1)[:, (i % 2) * 16:(i % 2 + 1) * 16, k:k + 1]
                            last = V.tensor_tensor(m1[:, i * 16:(i + 1) * 16, :],
                                                   p_b[(8 + i) % NPB][:, :].rearrange("p (v w) -> p v w", w=M1),
                                                   c.to_broadcast([P, 16, M1]), ALU.mult)
                            if k == 2:
                                last.then_inc(bank_free, 1)
                        link(last) if k < 2 else engine.wait_ge(bank_free, s.n(BANKS, 12))
                        ins = V.reduce_sum(red[:, h, M0:DX].rearrange("p (w k) -> p k w", k=3)[:, k, :],
                                           m1.rearrange("p v w -> p w v"), axis=AX_X)
                        link(ins)
                    engine.wait_ge(linear_done, s.n(1, 1))
                    link(V.tensor_tensor(red[:, h, :], red[:, h, :], p_m[:, 0:DX], ALU.add))
                    link(V.scalar_tensor_tensor(out=y[:, h, :], in0=xb[:, h, :], scalar=2.0, in1=red[:, h, :],
                                                op0=ALU.mult, op1=ALU.add))
                    link(V.bn_stats(bn[:, h, :], y[:, h, :]))
                    V.bn_aggr(mv[:, h, :], bn[:, h, :]).then_inc(mv_ready, 1)
                    assert links[0] == CH

                def final(s):
                    h = s.slot(2)
                    engine.wait_ge(dev_ready, s.n(1, 1))
                    engine.wait_ge(stored[h], s.turn(2, 16))
                    V.reciprocal(inv[:, h, :], dev[:, h, :]).then_inc(inv_done, 1)
                    engine.wait_ge(inv_done, s.n(1, 1))
                    V.tensor_scalar(fin[:, h, :], y[:, h, :], mv[:, h, 0:1], inv[:, h, :], ALU.subtract,
                                    ALU.mult).then_inc(fin_ready, 1)

                pipeline(dve, NBLK, 2, [(0, main), (1, final)])

            @block.sync
            def _(sp):
                engine = Waits(sp, woken["sp"])

                def store(s):
                    h = s.slot(2)
                    engine.wait_ge(fin_ready, s.n(1, 1))
                    sp.dma_start(out[bass.ds(s.n(P), P), :], fin[:, h, :]).then_inc(stored[h], 16)

                pipeline(sp, NBLK - 1, 2, [(0, store)])
                last = NBLK - 1
                engine.wait_ge(fin_ready, NBLK)
                sp.dma_start(out[last * P:N, :], fin[0:NLAST, last % 2, :]).then_inc(stored[last % 2], 16)
                for h in range(2):
                    engine.wait_ge(stored[h], 16 * len(range(h, NBLK, 2)))


def kernel(**inputs):
    import numpy as _np
    import concourse.bacc as _bacc
    from concourse import mybir as _mybir
    from concourse.bass_utils import run_bass_kernel_spmd as _run

    nc = _bacc.Bacc("TRN2", target_bir_lowering=False, num_devices=1)
    arrays, args = {}, {}
    for name in sorted(inputs):
        if name == "node_vec1":
            continue
        a = _np.ascontiguousarray(inputs[name])
        arrays[f"in_{name}_dram"] = a
        args[name] = nc.dram_tensor(f"in_{name}_dram", a.shape, _mybir.dt.from_np(a.dtype), kind="ExternalInput").ap()
    out = nc.dram_tensor("out_0_dram", (N, DX), _mybir.dt.float32, kind="ExternalOutput").ap()
    build(nc, args, out)
    r = _run(nc, [arrays], core_ids=[0])
    return r.results[0]["out_0_dram"]
```
